# Optimizing a Trainium2 kernel written in Bass

```python
import numpy as np
import jax
import jax.numpy as jnp

def _softmax(x, axis=-1):
    return jax.nn.softmax(x, axis=axis)

def _gelu(x):
    return jax.nn.gelu(x, approximate=True)

def _silu(x):
    return jax.nn.silu(x)

def _sigmoid(x):
    return jax.nn.sigmoid(x)

def _layernorm(x, axis=-1, eps=1e-05):
    m = jnp.mean(x, axis=axis, keepdims=True)
    v = jnp.var(x, axis=axis, keepdims=True)
    return (x - m) / jnp.sqrt(v + eps)

def _scatter_add(tgt, idx, src, axis=0):
    return tgt.at[idx].add(src)

def _segment_sum(src, seg, n):
    return jax.ops.segment_sum(src, seg, n)
kernel_name = 'mk_audio_tower_d1_tok_audfeat256_r4_dcadad'

def setup_inputs(seed: int=0):
    np.random.seed(seed)
    _w = jnp.asarray

    def _rec_inputs():
        import jax
        import jax.numpy as jnp
        _rk = jax.random.key(seed)
        x = 7.22013e-05 + 1.00017 * jax.random.normal(jax.random.fold_in(_rk, 1), (32, 256, 128), jnp.float32)
        return x
    x = _rec_inputs()

    def _L0_tok_setup():
        import jax, jax.numpy as jnp
        import numpy as np
        FILTER_SIZE = 8
        INPUT_DIM = 128
        KERNEL_SIZE = 64
        key = jax.random.key(seed)
        k1, k2, k3, k4 = jax.random.split(key, 4)
        user_batch = jax.random.normal(k1, (32, 512, INPUT_DIM), dtype=jnp.float32)
        filt = jax.random.uniform(k2, (FILTER_SIZE, INPUT_DIM), dtype=jnp.float32)
        W_k = jax.random.uniform(k3, (FILTER_SIZE * INPUT_DIM, KERNEL_SIZE), dtype=jnp.float32)
        b_k = jax.random.uniform(k4, (KERNEL_SIZE,), dtype=jnp.float32)
        return {'user_batch': user_batch, 'filt': filt, 'W_k': W_k, 'b_k': b_k}
    _L0_tok_all = _L0_tok_setup()
    _L0_tok_in = {k: v for k, v in _L0_tok_all.items() if k in ('filt', 'W_k', 'b_k')}
    del _L0_tok_all

    def _L0_attn_setup():
        import jax, jax.numpy as jnp
        import numpy as np
        import math
        B, S, D = (4, 1024, 64)
        key = jax.random.key(seed)
        ks = jax.random.split(key, 9)
        s = 1.0 / math.sqrt(D)
        return {'src': jax.random.normal(ks[0], (B, S, D), dtype=jnp.float32), 'Wq': jax.random.normal(ks[1], (D, D), dtype=jnp.float32) * s, 'bq': jax.random.normal(ks[2], (D,), dtype=jnp.float32) * s, 'Wk': jax.random.normal(ks[3], (D, D), dtype=jnp.float32) * s, 'bk': jax.random.normal(ks[4], (D,), dtype=jnp.float32) * s, 'Wv': jax.random.normal(ks[5], (D, D), dtype=jnp.float32) * s, 'bv': jax.random.normal(ks[6], (D,), dtype=jnp.float32) * s, 'Wo': jax.random.normal(ks[7], (D, D), dtype=jnp.float32) * s, 'bo': jax.random.normal(ks[8], (D,), dtype=jnp.float32) * s}
    _L0_attn_all = _L0_attn_setup()
    _L0_attn_in = {k: v for k, v in _L0_attn_all.items() if k in ('Wq', 'bq', 'Wk', 'bk', 'Wv', 'bv', 'Wo', 'bo')}
    del _L0_attn_all

    def _L0_ffn_setup():
        import jax, jax.numpy as jnp
        import numpy as np
        D_MODEL = 64
        EXPERT_DIM = 128
        NUM_EXPERTS = 8
        TOP_K = 2
        SEQ_LEN = 512
        BATCH = 2
        key = jax.random.key(seed)
        ks = jax.random.split(key, 8)
        s = 0.02
        x = jax.random.normal(ks[0], (SEQ_LEN, BATCH, D_MODEL), dtype=jnp.float32)
        Wg = jax.random.normal(ks[1], (D_MODEL, NUM_EXPERTS), dtype=jnp.float32) * s
        bg = jax.random.normal(ks[2], (NUM_EXPERTS,), dtype=jnp.float32) * s
        bias = jnp.zeros((NUM_EXPERTS,), dtype=jnp.float32)
        W1 = jax.random.normal(ks[3], (NUM_EXPERTS, D_MODEL, EXPERT_DIM), dtype=jnp.float32) * s
        b1 = jax.random.normal(ks[4], (NUM_EXPERTS, EXPERT_DIM), dtype=jnp.float32) * s
        W2 = jax.random.normal(ks[5], (NUM_EXPERTS, EXPERT_DIM, D_MODEL), dtype=jnp.float32) * s
        b2 = jax.random.normal(ks[6], (NUM_EXPERTS, D_MODEL), dtype=jnp.float32) * s
        return {'x': x, 'Wg': Wg, 'bg': bg, 'bias': bias, 'W1': W1, 'b1': b1, 'W2': W2, 'b2': b2}
    _L0_ffn_all = _L0_ffn_setup()
    _L0_ffn_in = {k: v for k, v in _L0_ffn_all.items() if k in ('Wg', 'bg', 'bias', 'W1', 'b1', 'W2', 'b2')}
    del _L0_ffn_all
    return {'x': x, 'L0_tok_filt': _L0_tok_in['filt'], 'L0_tok_W_k': _L0_tok_in['W_k'], 'L0_tok_b_k': _L0_tok_in['b_k'], 'L0_attn_Wq': _L0_attn_in['Wq'], 'L0_attn_bq': _L0_attn_in['bq'], 'L0_attn_Wk': _L0_attn_in['Wk'], 'L0_attn_bk': _L0_attn_in['bk'], 'L0_attn_Wv': _L0_attn_in['Wv'], 'L0_attn_bv': _L0_attn_in['bv'], 'L0_attn_Wo': _L0_attn_in['Wo'], 'L0_attn_bo': _L0_attn_in['bo'], 'L0_ffn_Wg': _L0_ffn_in['Wg'], 'L0_ffn_bg': _L0_ffn_in['bg'], 'L0_ffn_bias': _L0_ffn_in['bias'], 'L0_ffn_W1': _L0_ffn_in['W1'], 'L0_ffn_b1': _L0_ffn_in['b1'], 'L0_ffn_W2': _L0_ffn_in['W2'], 'L0_ffn_b2': _L0_ffn_in['b2']}

def reference(x, L0_tok_filt, L0_tok_W_k, L0_tok_b_k, L0_attn_Wq, L0_attn_bq, L0_attn_Wk, L0_attn_bk, L0_attn_Wv, L0_attn_bv, L0_attn_Wo, L0_attn_bo, L0_ffn_Wg, L0_ffn_bg, L0_ffn_bias, L0_ffn_W1, L0_ffn_b1, L0_ffn_W2, L0_ffn_b2):
    import jax
    import jax.numpy as jnp

    def _L0_tok_ref(user_batch, filt, W_k, b_k):
        import jax, jax.numpy as jnp
        import numpy as np
        FILTER_SIZE = 8
        INPUT_DIM = 128
        KERNEL_SIZE = 64
        B, L, D = user_batch.shape
        F = filt.shape[0]
        n_win = L - F
        idx = jnp.arange(n_win)[:, None] + jnp.arange(F)[None, :]
        windows = user_batch[:, idx, :]
        W = W_k.reshape(F, D, -1)
        out = jnp.einsum('blfd,fd,fdk->blk', windows, filt, W)
        return jax.nn.relu(out + b_k)

    def _L0_attn_ref(src, Wq, bq, Wk, bk, Wv, bv, Wo, bo):
        import jax, jax.numpy as jnp
        import numpy as np
        import math
        B, S, D = (4, 1024, 64)
        q = src @ Wq.T + bq
        k = src @ Wk.T + bk
        v = src @ Wv.T + bv
        row_mask = (q[:, :, 0] != 0) & (k[:, :, 0] != 0)
        mask = row_mask[:, :, None]
        scale = 1.0 / math.sqrt(D)
        scores = jnp.einsum('bid,bjd->bij', q, k) * scale
        scores = jnp.where(mask, scores, jnp.float32(-1000000000.0))
        prob = jax.nn.softmax(scores, axis=-1)
        prob = jnp.where(mask, prob, 0.0)
        out = jnp.einsum('bij,bjd->bid', prob, v)
        return out @ Wo.T + bo

    def _L0_ffn_ref(x, Wg, bg, bias, W1, b1, W2, b2):
        import jax, jax.numpy as jnp
        import numpy as np
        D_MODEL = 64
        EXPERT_DIM = 128
        NUM_EXPERTS = 8
        TOP_K = 2
        SEQ_LEN = 512
        BATCH = 2
        x_flat = x.reshape(-1, D_MODEL)
        gate_logits = x_flat @ Wg + bg + bias
        topk_vals, topk_idx = jax.lax.top_k(gate_logits, TOP_K)
        topk_w = jax.nn.softmax(topk_vals, axis=-1)
        combine = (jax.nn.one_hot(topk_idx, NUM_EXPERTS, dtype=x.dtype) * topk_w[..., None]).sum(axis=1)
        h = jax.nn.relu(jnp.einsum('td,edh->teh', x_flat, W1) + b1)
        y = jnp.einsum('teh,ehd->ted', h, W2) + b2
        out = jnp.einsum('ted,te->td', y, combine)
        return out.reshape(x.shape)
    h = _L0_tok_ref(x, L0_tok_filt, L0_tok_W_k, L0_tok_b_k)
    h = h + _L0_attn_ref(_layernorm(h, axis=-1), L0_attn_Wq, L0_attn_bq, L0_attn_Wk, L0_attn_bk, L0_attn_Wv, L0_attn_bv, L0_attn_Wo, L0_attn_bo)
    h = h + _L0_ffn_ref(_layernorm(h, axis=-1), L0_ffn_Wg, L0_ffn_bg, L0_ffn_bias, L0_ffn_W1, L0_ffn_b1, L0_ffn_W2, L0_ffn_b2)
    return h

_drawn_inputs = setup_inputs


def setup_inputs(seed=0):
    import zlib

    import numpy as np

    out = dict(_drawn_inputs(seed))
    spreads = {'L0_ffn_bias': (0.0, 0.8)}
    factors = {'L0_attn_Wq': 3.194,
     'L0_attn_bq': 8.0,
     'L0_attn_Wk': 3.243,
     'L0_attn_bk': 64.0,
     'L0_attn_Wv': 2.801,
     'L0_attn_bv': 2.908,
     'L0_attn_bo': 3.864,
     'L0_ffn_Wg': 8.0,
     'L0_ffn_bg': 22.538,
     'L0_ffn_W1': 8.0,
     'L0_ffn_b1': 24.531,
     'L0_ffn_W2': 8.0,
     'L0_ffn_b2': 31.624}
    for name, (base, spread) in spreads.items():
        noise = np.random.default_rng([zlib.crc32(name.encode()), seed]).standard_normal(out[name].shape)
        drawn = base * np.exp(spread * noise) if base else spread * noise
        out[name] = jnp.asarray(drawn.astype(out[name].dtype))
    for name, factor in factors.items():
        out[name] = (out[name] * factor).astype(out[name].dtype)
    return out
```

```python
from contextlib import ExitStack

import numpy as np
import concourse.bass as bass
from concourse import mybir

F32 = mybir.dt.float32
F32R = mybir.dt.float32r
U32 = mybir.dt.uint32
ALU = mybir.AluOpType
ACT = mybir.ActivationFunctionType
AX = mybir.AxisListType

SEQS, LEN, DIN = 32, 256, 128
TAPS, D = 8, 64
WIN = LEN - TAPS
HALF = WIN // 2
PAIR = 2
GROUPS = SEQS // PAIR
TOK = PAIR * WIN
EXPERTS, HID = 8, 128
EPAIRS = EXPERTS // 2
CHUNKS = 2 * PAIR
VCOLS = PAIR * D + 4
EPS = 1e-5
EXP_LN_SET = 6
QSCALE = D ** -0.5

C_BTOK, C_BQ, C_BK, C_BO, C_B1, C_B2, C_FILT, C_BV = 0, 1, 2, 3, 4, 12, 16, 24
NCOLS = 25
R_BG, R_BIAS, R_QK0, R_IOTA = 0, 32, 64, 68
NROWS = 100
K_ID, K_CENTER, K_MEAN, K_FOLD, K_SEL = 0, 128, 256, 384, 448
NCONST = K_SEL + EPAIRS * 128


def audio_tower(nc, xt, wtok, cols, rows, const, bdq, bdk, wv, wot, bdg, w1, w2, out):
    ctx = ExitStack()
    with ctx:
        def sb(name, shape, dt=F32):
            return ctx.enter_context(nc.sbuf_tensor(name, shape, dt))

        def bank(name):
            return ctx.enter_context(nc.psum_tensor(name, [128, 512], F32))

        def sem(name):
            return ctx.enter_context(nc.semaphore(name))

        wtok_sb = sb("wtok_sb", [128, TAPS, D])
        wconv = sb("wconv", [128, TAPS, D])
        col = sb("col", [128, NCOLS])
        row = sb("row", [128, NROWS])
        cst = sb("cst", [128, NCONST])
        sel = sb("sel", [16, EPAIRS, 128], F32R)
        bq_scaled = sb("bq_scaled", [128, 1])
        eps = sb("eps", [128, 1])
        wq_sb = sb("wq_sb", [128, 128])
        wk_sb = sb("wk_sb", [128, 128])
        wv_sb = sb("wv_sb", [D, D])
        wot_sb = sb("wot_sb", [D, D])
        bv_wide = sb("bv_wide", [D, 128])
        wval = sb("wval", [128, VCOLS])
        bval = sb("bval", [128, VCOLS])
        wg_sb = sb("wg_sb", [128, 2 * EXPERTS])
        w1_sb = sb("w1_sb", [128, EXPERTS, HID])
        w1_hi = sb("w1_hi", [128, EXPERTS, HID], F32R)
        w1_lo = sb("w1_lo", [128, EXPERTS, HID], F32R)
        w2_sb = sb("w2_sb", [HID, EXPERTS, D])
        ident = cst[:, K_ID:K_ID + 128]
        center = cst[:, K_CENTER:K_CENTER + 128]
        meanof = cst[:, K_MEAN:K_MEAN + 128]
        fold = cst[:, K_FOLD:K_FOLD + D]

        x_sb = [sb(f"x{i}", [128, PAIR, LEN]) for i in range(2)]
        h = [sb(f"h{i}", [128, WIN]) for i in range(2)]
        h2 = [sb(f"h2_{i}", [128, WIN]) for i in range(2)]
        sq = [sb(f"sq{i}", [128, WIN]) for i in range(2)]
        lnv = [sb(f"lnv{i}", [128, WIN]) for i in range(2)]
        rstd = [sb(f"rstd{i}", [128, WIN]) for i in range(2)]
        xn = sb("xn", [128, WIN])
        xn2 = sb("xn2", [128, WIN])
        qpad = sb("qpad", [128, PAIR, WIN])
        k_sb = sb("k_sb", [128, WIN])
        v_sb = sb("v_sb", [128, 2, VCOLS])
        kmask = sb("kmask", [128, 2, PAIR])
        mask = sb("mask", [128, 2, PAIR])
        nmax = sb("nmax", [128, PAIR, 2])
        psum_p = sb("psum_p", [128, PAIR, 2])
        rsum = sb("rsum", [128, PAIR, 2])
        rmask = sb("rmask", [128, PAIR, 2])
        p_sb = [sb(f"p{b}", [128, 2, WIN]) for b in range(PAIR)]
        pt_sb = [sb(f"pt{b}", [128, 2, WIN]) for b in range(PAIR)]
        xs = [sb(f"xs{i}", [128, TOK], F32R) for i in range(2)]
        lg1 = sb("lg1", [128, CHUNKS, EXPERTS])
        lg = sb("lg", [128, CHUNKS, EXPERTS])
        top = sb("top", [128, CHUNKS, 8])
        topi = sb("topi", [128, CHUNKS, 8], U32)
        topf = sb("topf", [128, CHUNKS, 2])
        dlt = sb("dlt", [128, CHUNKS])
        eg = sb("eg", [128, CHUNKS])
        den = sb("den", [128, CHUNKS])
        gw1 = sb("gw1", [128, CHUNKS])
        gw2 = sb("gw2", [128, CHUNKS])
        oh1 = sb("oh1", [128, CHUNKS, EXPERTS])
        oh2 = sb("oh2", [128, CHUNKS, EXPERTS])
        cw1 = sb("cw1", [128, CHUNKS, EXPERTS])
        cw2 = sb("cw2", [128, CHUNKS, EXPERTS])
        cw = sb("cw", [128, CHUNKS, EXPERTS])
        cwhl = sb("cwhl", [128, CHUNKS, 2 * EXPERTS], F32R)
        ct_sb = sb("ct_sb", [16, TOK], F32R)
        hid = [sb(f"hid{i}", [128, TOK]) for i in range(4)]
        y_sb = [sb(f"y{i}", [128, TOK]) for i in range(2)]
        acc = [sb(f"acc{i}", [128, TOK]) for i in range(2)]
        total = sb("total", [128, TOK])
        o_sb = [sb(f"o{i}", [128, WIN]) for i in range(2)]

        bank_h = [bank("bank_h0"), bank("bank_h1")]
        bank_y = bank("bank_y")
        bank_c = bank("bank_c")
        bank_s = [bank("bank_s0"), bank("bank_s1")]
        bank_a = bank("bank_a")
        bank_b = bank("bank_b")

        par_in = sem("par_in")
        set_pool = sem("set_pool")
        set_dve = sem("set_dve")
        set_pe = sem("set_pe")
        x_in = [sem("x_in0"), sem("x_in1")]
        o_out = [sem("o_out0"), sem("o_out1")]
        passed = sem("passed")
        conv_done = sem("conv_done")
        h_ready = sem("h_ready")
        cen = [sem("cen1"), sem("cen2")]
        sqr = [sem("sqr1"), sem("sqr2")]
        var = [sem("var1"), sem("var2")]
        lnd = [sem("lnd1"), sem("lnd2")]
        rsd = [sem("rsd1"), sem("rsd2")]
        xn_ready = sem("xn_ready")
        xn2_ready = sem("xn2_ready")
        q_done = sem("q_done")
        kv_done = sem("kv_done")
        q_ready = sem("q_ready")
        kv_ready = sem("kv_ready")
        kmask_ready = sem("kmask_ready")
        mask_ready = sem("mask_ready")
        sc_done = sem("sc_done")
        nmax_ready = sem("nmax_ready")
        ex_ready = sem("ex_ready")
        rs_ready = sem("rs_ready")
        rm_ready = sem("rm_ready")
        p_ready = sem("p_ready")
        pt_done = sem("pt_done")
        pt_ready = [sem("pt_ready0"), sem("pt_ready1")]
        pv_done = sem("pv_done")
        h2_ready = sem("h2_ready")
        xhi = sem("xhi")
        xlo = sem("xlo")
        gate_done = sem("gate_done")
        topk = sem("topk")
        dlt_ready = sem("dlt_ready")
        eg_ready = sem("eg_ready")
        cw_ready = sem("cw_ready")
        ct_done = sem("ct_done")
        ct_ready = sem("ct_ready")
        l1_done = sem("l1_done")
        hid_ready = [sem("hid_even"), sem("hid_odd")]
        y_done = sem("y_done")
        y_ready = sem("y_ready")
        cb_done = sem("cb_done")
        acc_ready = sem("acc_ready")
        sum_ready = sem("sum_ready")
        fin_done = sem("fin_done")
        out_ready = sem("out_ready")

        N_PAR = 12

        def after(eng, s, value):
            if not isinstance(value, int) or value > 0:
                eng.wait_ge(s, value)

        def hold(eng, s, value):
            eng.wait_ge(s, value)
            eng.sem_inc(passed, 1)

        def run(eng, iteration):
            iteration(-1, 1, True, False, False, False)
            iteration(0, 0, True, True, False, False)
            iteration(1, 1, True, True, True, False)
            iteration(2, 0, True, True, True, True)
            with eng.Fori(0, (GROUPS - 4) // 2) as i:
                iteration(i * 2 + 3, 1, True, True, True, True)
                iteration(i * 2 + 4, 0, True, True, True, True)
            iteration(GROUPS - 1, 1, False, True, True, True)
            iteration(GROUPS, 0, False, False, True, True)
            iteration(GROUPS + 1, 1, False, False, False, True)

        block = ctx.enter_context(nc.Block())

        @block.sync
        def _(sp):
            for dst, src in ((wtok_sb[:, :, :], wtok), (col[:, :], cols), (cst[:, :], const)):
                sp.dma_start(dst, src).then_inc(par_in, 16)
            for dst, src in ((row[:, :], rows), (wq_sb[:, :], bdq), (wk_sb[:, :], bdk), (wv_sb[:, :], wv),
                             (wot_sb[:, :], wot), (wg_sb[:, :], bdg), (w2_sb[:, :, :], w2),
                             (w1_sb[0:D, :, :], w1), (w1_sb[D:128, :, :], w1)):
                sp.dma_start(dst, src).then_inc(par_in, 16)

            def iteration(t, odd, conv, attn, moe, fin):
                if conv:
                    c = t + 1
                    after(sp, conv_done, c - 1)
                    sp.dma_start(x_sb[1 - odd][:, :, :], xt[c]).then_inc(x_in[1 - odd], 16)
                if fin:
                    f = t - 2
                    sp.wait_ge(out_ready, f + 1)
                    sp.dma_start(out[f], o_sb[odd][:, :]).then_inc(o_out[odd], 16)

            run(sp, iteration)
            for i in range(2):
                sp.wait_ge(o_out[i], 16 * GROUPS // 2)

        @block.gpsimd
        def _(pool):
            pool.memset(qpad[:, :, :], 0.0)
            pool.memset(eps[:, :], EPS).then_inc(set_pool, 1)

            def scale(n, b):
                hold(pool, rm_ready, 2 * n + b + 1)
                for i in range(2):
                    last = pool.tensor_scalar(p_sb[b][0:HALF, i, :], p_sb[b][0:HALF, i, :],
                                              rmask[0:HALF, b, i:i + 1], None, ALU.mult)
                last.then_inc(p_ready, 1)

            def add(m, p):
                pool.wait_ge(acc_ready, 4 * m + p + 1)
                if p == 1:
                    after(pool, fin_done, m)
                    pool.tensor_tensor(total[:, :], acc[0][:, :], acc[1][:, :], ALU.add).then_inc(sum_ready, 1)
                else:
                    pool.wait_ge(sum_ready, 3 * m + p - 1)
                    pool.tensor_tensor(total[:, :], total[:, :], acc[p % 2][:, :], ALU.add).then_inc(sum_ready, 1)

            def iteration(t, odd, conv, attn, moe, fin):
                n, m = t, t - 1
                if attn:
                    scale(n, 0)
                    scale(n, 1)
                if moe:
                    for p in range(1, EPAIRS):
                        add(m, p)

            run(pool, iteration)

        @block.scalar
        def _(act):
            act.add_instruction(mybir.InstLoadActFuncSet(name=nc.get_next_instruction_name(), engine=mybir.EngineType.Activation,
                                                         ins=[], outs=[], act_func_set_id=EXP_LN_SET))
            act.wait_ge(par_in, 16 * N_PAR)
            act.wait_ge(set_pool, 1)
            act.wait_ge(set_dve, 1)

            def exps(n, b):
                act.wait_ge(nmax_ready, 2 * n + b + 1)
                after(act, pt_done, 2 * n + b - 1)
                after(act, rs_ready, 2 * n + b - 1)
                for i in range(2):
                    last = act.activation(p_sb[b][0:HALF, i, :], bank_s[b][0:HALF, i * WIN:(i + 1) * WIN], ACT.Exp,
                                          bias=nmax[0:HALF, b, i:i + 1], accum_out=psum_p[0:HALF, b, i:i + 1])
                last.then_inc(ex_ready, 1)

            def relu_even(m, p):
                act.wait_ge(l1_done, 8 * m + 2 * p + 1)
                after(act, y_done, 4 * m + p - 1)
                act.activation(hid[2 * (p % 2)][:, :], bank_h[0][:, 0:TOK], ACT.Relu,
                               bias=col[:, C_B1 + 2 * p:C_B1 + 2 * p + 1]).then_inc(hid_ready[0], 1)

            def y_out(m, p):
                act.wait_ge(y_done, 4 * m + p + 1)
                after(act, acc_ready, 4 * m + p - 1)
                act.activation(y_sb[p % 2][:, :], bank_y[:, 0:TOK], ACT.Identity,
                               bias=col[:, C_B2 + p:C_B2 + p + 1]).then_inc(y_ready, 1)

            def square(g, which, src):
                act.wait_ge(cen[which], g + 1)
                after(act, var[which], g)
                act.activation(sq[which][:, :], src[:, 0:WIN], ACT.Square).then_inc(sqr[which], 1)

            def rsqrt(g, which, src, used):
                act.wait_ge(var[which], g + 1)
                act.activation(lnv[which][:, :], src[:, WIN:2 * WIN], ACT.Ln, bias=eps[:, :]).then_inc(lnd[which], 1)
                act.wait_ge(lnd[which], g + 1)
                after(act, used, g)
                act.activation(rstd[which][:, :], lnv[which][:, :], ACT.Exp, scale=-0.5).then_inc(rsd[which], 1)

            def iteration(t, odd, conv, attn, moe, fin):
                c, n, m = t + 1, t, t - 1
                even = 1 - odd
                if attn:
                    exps(n, 0)
                if moe:
                    relu_even(m, 0)
                if attn:
                    exps(n, 1)
                if moe:
                    y_out(m, 0)
                if conv:
                    act.wait_ge(conv_done, c + 1)
                    after(act, h2_ready, n)
                    act.activation(h[even][:, :], bank_a[:, 0:WIN], ACT.Relu,
                                   bias=col[:, C_BTOK:C_BTOK + 1]).then_inc(h_ready, 1)
                if attn:
                    act.wait_ge(pt_done, 2 * n + 1)
                    after(act, pv_done, n)
                    act.activation(pt_sb[0][0:HALF, :, :],
                                   bank_s[0][0:HALF, 0:TOK].rearrange("p (a b) -> p a b", a=2),
                                   ACT.Copy).then_inc(pt_ready[0], 1)
                if moe:
                    relu_even(m, 1)
                if conv:
                    square(c, 0, bank_b)
                if moe:
                    y_out(m, 1)
                if conv:
                    rsqrt(c, 0, bank_b, xn_ready)
                if moe:
                    relu_even(m, 2)
                if attn:
                    square(n, 1, bank_a)
                if moe:
                    y_out(m, 2)
                if attn:
                    rsqrt(n, 1, bank_a, xn2_ready)
                if conv:
                    act.wait_ge(q_done, c + 1)
                    after(act, sc_done, 2 * c)
                    for b in range(PAIR):
                        rows_b = slice(b * D, b * D + D)
                        last = act.activation(qpad[rows_b, b, :], bank_b[rows_b, 0:WIN], ACT.Identity,
                                              bias=bq_scaled[rows_b, :], scale=QSCALE)
                    last.then_inc(q_ready, 1)
                if moe:
                    relu_even(m, 3)
                if attn:
                    act.wait_ge(xn2_ready, n + 1)
                    after(act, l1_done, 8 * m)
                    act.activation(xs[odd][0:D, 0:WIN], xn2[0:D, :], ACT.Copy)
                    act.activation(xs[odd][D:128, WIN:TOK], xn2[D:128, :], ACT.Copy).then_inc(xhi, 1)
                if moe:
                    y_out(m, 3)
                if attn:
                    act.wait_ge(dlt_ready, n + 1)
                    act.activation(eg[0:HALF, :], dlt[0:HALF, :], ACT.Exp).then_inc(eg_ready, 1)

            run(act, iteration)

        @block.vector
        def _(dve):
            dve.wait_ge(par_in, 16 * N_PAR)
            dve.tensor_scalar(bq_scaled[:, :], col[:, C_BQ:C_BQ + 1], QSCALE, None, ALU.mult)
            dve.tensor_tensor(wconv[:, :, :], wtok_sb[:, :, :],
                              col[:, C_FILT:C_FILT + TAPS].unsqueeze(2).to_broadcast([128, TAPS, D]),
                              ALU.mult).then_inc(set_dve, 1)
            dve.tensor_copy(w1_hi[:, :, :], w1_sb[:, :, :]).then_inc(set_dve, 1)
            dve.tensor_copy(bv_wide[:, :], col[0:D, C_BV:C_BV + 1].to_broadcast([D, 128])).then_inc(set_dve, 1)
            dve.wait_ge(set_dve, 2)
            dve.tensor_tensor(w1_lo[:, :, :], w1_sb[:, :, :], w1_hi[:, :, :].bitcast(F32), ALU.subtract)
            dve.tensor_copy(sel[:, :, :], cst[0:16, K_SEL:NCONST].rearrange("p (a b) -> p a b", a=EPAIRS))
            dve.memset(wval[:, :], 0.0).then_inc(set_dve, 1)
            dve.wait_ge(set_dve, 4)
            for j in range(2):
                dve.tensor_copy(wval[:, 128 + j:129 + j], wq_sb[:, j * D:j * D + 1])
                dve.tensor_copy(wval[:, 130 + j:131 + j], wk_sb[:, j * D:j * D + 1])
            dve.wait_ge(set_pe, 1)
            for b in range(PAIR):
                rows_b = slice(b * D, b * D + D)
                dve.tensor_copy(wval[rows_b, b * D:b * D + D], bank_a[rows_b, 0:D])
                dve.tensor_copy(bval[:, b * D:b * D + D], bank_a[:, D:2 * D])
            dve.tensor_copy(bval[:, PAIR * D:VCOLS], row[:, R_QK0:R_QK0 + 4]).then_inc(set_dve, 1)

            def relu_odd(m, p):
                dve.wait_ge(l1_done, 8 * m + 2 * p + 2)
                after(dve, y_done, 4 * m + p - 1)
                dve.tensor_scalar(hid[2 * (p % 2) + 1][:, :], bank_h[1][:, 0:TOK],
                                  col[:, C_B1 + 2 * p + 1:C_B1 + 2 * p + 2], 0.0, ALU.add,
                                  ALU.max).then_inc(hid_ready[1], 1)

            def weigh(m, p):
                dve.wait_ge(y_ready, 4 * m + p + 1)
                dve.wait_ge(cb_done, 4 * m + p + 1)
                after(dve, sum_ready, 3 * m + (-1, 0, 1, 1)[p])
                dve.tensor_tensor(acc[p % 2][:, :], y_sb[p % 2][:, :], bank_c[:, 0:TOK],
                                  ALU.mult).then_inc(acc_ready, 1)

            def rowmax(n, b):
                dve.wait_ge(sc_done, 2 * n + b + 1)
                after(dve, ex_ready, 2 * n + b - 1)
                dve.tensor_reduce(nmax[0:HALF, b, :], bank_s[b][0:HALF, 0:TOK].rearrange("p (a b) -> p a b", a=2),
                                  AX.X, ALU.max, negate=True).then_inc(nmax_ready, 1)

            def recip(n, b):
                dve.wait_ge(ex_ready, 2 * n + b + 1)
                after(dve, p_ready, 2 * n + b - 1)
                dve.reciprocal(rsum[0:HALF, b, :], psum_p[0:HALF, b, :]).then_inc(rs_ready, 1)
                dve.wait_ge(rs_ready, 2 * n + b + 1)
                dve.wait_ge(mask_ready, n + 1)
                dve.tensor_tensor(rmask[0:HALF, b, :], rsum[0:HALF, b, :], mask[0:HALF, :, b],
                                  ALU.mult).then_inc(rm_ready, 1)

            def choose(n):
                T = slice(0, HALF)

                def seen(k):
                    dve.wait_ge(topk, 12 * n + k)

                def wide(a):
                    return a.unsqueeze(2).to_broadcast([HALF, CHUNKS, EXPERTS])

                dve.wait_ge(gate_done, n + 1)
                dve.tensor_tensor(lg1[T, :, :], bank_a[T, 0:CHUNKS * EXPERTS].rearrange("p (a b) -> p a b", a=CHUNKS),
                                  row[T, R_BG:R_BG + 32].rearrange("p (a b) -> p a b", a=CHUNKS),
                                  ALU.add).then_inc(topk, 1)
                seen(1)
                dve.tensor_tensor(lg[T, :, :], lg1[T, :, :],
                                  row[T, R_BIAS:R_BIAS + 32].rearrange("p (a b) -> p a b", a=CHUNKS),
                                  ALU.add).then_inc(topk, 1)
                hold(dve, topk, 12 * n + 2)
                for j in range(CHUNKS):
                    last = dve.max(top[T, j, :], lg[T, j, :])
                last.then_inc(topk, 1)
                seen(3)
                dve.tensor_tensor(dlt[T, :], top[T, :, 1], top[T, :, 0], ALU.subtract).then_inc(dlt_ready, 1)
                for j in range(CHUNKS):
                    last = dve.max_index(topi[T, j, :], top[T, j, :], lg[T, j, :])
                last.then_inc(topk, 1)
                seen(4)
                dve.tensor_copy(topf[T, :, :], topi[T, :, 0:2]).then_inc(topk, 1)
                seen(5)
                iota = row[T, R_IOTA:R_IOTA + 32].rearrange("p (a b) -> p a b", a=CHUNKS)
                dve.tensor_tensor(oh1[T, :, :], iota, wide(topf[T, :, 0]), ALU.is_equal)
                dve.tensor_tensor(oh2[T, :, :], iota, wide(topf[T, :, 1]), ALU.is_equal).then_inc(topk, 1)
                dve.wait_ge(eg_ready, n + 1)
                dve.tensor_scalar(den[T, :], eg[T, :], 1.0, None, ALU.add).then_inc(topk, 1)
                seen(7)
                dve.reciprocal(gw1[T, :], den[T, :]).then_inc(topk, 1)
                seen(8)
                dve.tensor_tensor(gw2[T, :], eg[T, :], gw1[T, :], ALU.mult).then_inc(topk, 1)
                dve.tensor_tensor(cw1[T, :, :], oh1[T, :, :], wide(gw1[T, :]), ALU.mult)
                seen(9)
                dve.tensor_tensor(cw2[T, :, :], oh2[T, :, :], wide(gw2[T, :]), ALU.mult).then_inc(topk, 1)
                seen(10)
                dve.tensor_tensor(cw[T, :, :], cw1[T, :, :], cw2[T, :, :], ALU.add).then_inc(topk, 1)
                seen(11)
                after(dve, ct_done, n)
                dve.tensor_copy(cwhl[T, :, 0:EXPERTS], cw[T, :, :]).then_inc(topk, 1)
                seen(12)
                dve.tensor_tensor(cwhl[T, :, EXPERTS:], cw[T, :, :], cwhl[T, :, 0:EXPERTS].bitcast(F32),
                                  ALU.subtract).then_inc(cw_ready, 1)

            def iteration(t, odd, conv, attn, moe, fin):
                c, n, m, f = t + 1, t, t - 1, t - 2
                even = 1 - odd
                if attn:
                    rowmax(n, 0)
                    rowmax(n, 1)
                if moe:
                    dve.wait_ge(ct_done, m + 1)
                    after(dve, cb_done, 4 * m)
                    dve.tensor_copy(ct_sb[:, :], bank_b[0:16, 0:TOK]).then_inc(ct_ready, 1)
                    relu_odd(m, 0)
                if attn:
                    recip(n, 0)
                if moe:
                    weigh(m, 0)
                if attn:
                    recip(n, 1)
                if fin:
                    dve.wait_ge(fin_done, f + 1)
                    after(dve, o_out[odd], 8 * (f - odd))
                    dve.tensor_tensor(o_sb[odd][:, :], bank_b[:, 0:WIN], h2[odd][:, :],
                                      ALU.add).then_inc(out_ready, 1)
                if moe:
                    relu_odd(m, 1)
                if attn:
                    dve.wait_ge(pt_done, 2 * n + 2)
                    after(dve, pv_done, n)
                    dve.tensor_copy(pt_sb[1][0:HALF, :, :],
                                    bank_s[1][0:HALF, 0:TOK].rearrange("p (a b) -> p a b", a=2)
                                    ).then_inc(pt_ready[1], 1)
                if moe:
                    weigh(m, 1)
                if attn:
                    dve.wait_ge(pv_done, n + 1)
                    dve.scalar_tensor_tensor(out=h2[odd][:, :], in0=bank_a[:, 0:WIN],
                                             scalar=col[:, C_BO:C_BO + 1], in1=h[odd][:, :], op0=ALU.add,
                                             op1=ALU.add).then_inc(h2_ready, 1)
                if conv:
                    dve.wait_ge(rsd[0], c + 1)
                    after(dve, kv_done, c)
                    dve.tensor_tensor(xn[:, :], bank_b[:, 0:WIN], rstd[0][:, :], ALU.mult).then_inc(xn_ready, 1)
                if moe:
                    relu_odd(m, 2)
                    weigh(m, 2)
                if attn:
                    dve.wait_ge(rsd[1], n + 1)
                    after(dve, gate_done, n)
                    after(dve, xhi, n)
                    dve.tensor_tensor(xn2[:, :], bank_a[:, 0:WIN], rstd[1][:, :], ALU.mult).then_inc(xn2_ready, 1)
                if moe:
                    relu_odd(m, 3)
                if conv:
                    dve.wait_ge(kv_done, c + 1)
                    after(dve, sc_done, 2 * c)
                    dve.tensor_scalar(k_sb[:, :], bank_s[0][:, 0:WIN], col[:, C_BK:C_BK + 1], None, ALU.add)
                    after(dve, pv_done, c)
                    dve.tensor_tensor(v_sb[0:HALF, :, :],
                                      bank_s[0][0:HALF, WIN:WIN + 2 * VCOLS].rearrange("p (a b) -> p a b", a=2),
                                      bval[0:HALF, :].unsqueeze(1).to_broadcast([HALF, 2, VCOLS]),
                                      ALU.add).then_inc(kv_ready, 1)
                    dve.wait_ge(kv_ready, c + 1)
                    dve.tensor_scalar(kmask[0:HALF, :, :], v_sb[0:HALF, :, 130:132], 0.0, None,
                                      ALU.not_equal).then_inc(kmask_ready, 1)
                    dve.wait_ge(kmask_ready, c + 1)
                    dve.scalar_tensor_tensor(out=mask[0:HALF, :, :], in0=v_sb[0:HALF, :, 128:130], scalar=0.0,
                                             in1=kmask[0:HALF, :, :], op0=ALU.not_equal,
                                             op1=ALU.mult).then_inc(mask_ready, 1)
                if attn:
                    dve.wait_ge(xhi, n + 1)
                    dve.tensor_tensor(xs[odd][D:128, 0:WIN], xn2[0:D, :], xs[odd][0:D, 0:WIN].bitcast(F32),
                                      ALU.subtract)
                    dve.tensor_tensor(xs[odd][0:D, WIN:TOK], xn2[D:128, :], xs[odd][D:128, WIN:TOK].bitcast(F32),
                                      ALU.subtract).then_inc(xlo, 1)
                    choose(n)
                if moe:
                    weigh(m, 3)

            run(dve, iteration)

        @block.tensor
        def _(pe):
            def conv_taps(c, par, taps):
                for j in taps:
                    for b in range(PAIR):
                        last = pe.matmul(bank_a[b * D:b * D + D, 0:WIN], wconv[:, j, :], x_sb[par][:, b, j:j + WIN],
                                         start=(j == 0), stop=(j == TAPS - 1))
                if TAPS - 1 in taps:
                    last.then_inc(conv_done, 1)

            def scores(n, b):
                for i in range(2):
                    last = pe.matmul(bank_s[b][0:HALF, i * WIN:(i + 1) * WIN], qpad[:, b, i * HALF:(i + 1) * HALF],
                                     k_sb[:, :], start=True, stop=True)
                last.then_inc(sc_done, 1)

            def turn_p(n, b):
                pe.wait_ge(p_ready, 2 * n + b + 1)
                for j in range(2):
                    for i in range(2):
                        at = j * WIN + i * HALF
                        last = pe.transpose(bank_s[b][0:HALF, at:at + HALF],
                                            p_sb[b][0:HALF, i, j * HALF:(j + 1) * HALF], ident[0:HALF, 0:HALF])
                last.then_inc(pt_done, 1)

            def turn_weights(m):
                pe.wait_ge(cw_ready, m + 1)
                for j in range(CHUNKS):
                    i, b = j // PAIR, j % PAIR
                    at = b * WIN + i * HALF
                    last = pe.transpose(bank_b[0:16, at:at + HALF], cwhl[0:HALF, j, :].bitcast(F32),
                                        ident[0:HALF, 0:HALF])
                last.then_inc(ct_done, 1)

            def hidden(m, par, p):
                for e in (2 * p, 2 * p + 1):
                    after(pe, hid_ready[e % 2], 4 * m + p)
                    pe.matmul(bank_h[e % 2][:, 0:TOK], w1_hi[:, e, :], xs[par][:, :], start=True, stop=False)
                    pe.matmul(bank_h[e % 2][:, 0:TOK], w1_lo[:, e, :], xs[par][:, :], start=False,
                              stop=True).then_inc(l1_done, 1)

            def expert_out(m, p):
                pe.wait_ge(hid_ready[0], 4 * m + p + 1)
                pe.wait_ge(hid_ready[1], 4 * m + p + 1)
                after(pe, y_ready, 4 * m + p)
                for s in range(2):
                    last = pe.matmul(bank_y[s * D:s * D + D, 0:TOK], w2_sb[:, 2 * p + s, :],
                                     hid[2 * (p % 2) + s][:, :], start=True, stop=True)
                last.then_inc(y_done, 1)
                after(pe, acc_ready, 4 * m + p)
                if p == 0:
                    pe.wait_ge(ct_ready, m + 1)
                pe.matmul(bank_c[:, 0:TOK], sel[:, p, :], ct_sb[:, :], start=True, stop=True).then_inc(cb_done, 1)

            def centre(g, which, dst, src):
                pe.matmul(dst[:, 0:WIN], center, src[:, :], start=True, stop=True).then_inc(cen[which], 1)

            def variance(g, which, dst):
                pe.wait_ge(sqr[which], g + 1)
                pe.matmul(dst[:, WIN:2 * WIN], meanof, sq[which][:, :], start=True, stop=True).then_inc(var[which], 1)

            pe.wait_ge(par_in, 16 * N_PAR)
            pe.wait_ge(set_dve, 3)
            for b in range(PAIR):
                pe.matmul(bank_a[b * D:b * D + D, 0:D], wv_sb[:, :], wot_sb[:, :], start=True, stop=True)
            pe.matmul(bank_a[:, D:2 * D], bv_wide[:, :], wot_sb[:, :], start=True, stop=True).then_inc(set_pe, 1)
            pe.wait_ge(set_dve, 5)

            def iteration(t, odd, conv, attn, moe, fin):
                c, n, m, f = t + 1, t, t - 1, t - 2
                even = 1 - odd
                if attn:
                    pe.wait_ge(q_ready, n + 1)
                    pe.wait_ge(kv_ready, n + 1)
                    after(pe, pt_ready[0], n)
                    scores(n, 0)
                    after(pe, pt_ready[1], n)
                    scores(n, 1)
                if moe:
                    after(pe, out_ready, t - 2)
                    turn_weights(m)
                    pe.wait_ge(xhi, m + 1)
                    pe.wait_ge(xlo, m + 1)
                    hidden(m, even, 0)
                if conv or attn:
                    after(pe, topk, 12 * (n - 1) + 1)
                if conv:
                    pe.wait_ge(x_in[even], 8 * (c - even) + 16)
                    conv_taps(c, even, range(0, 4))
                if moe:
                    expert_out(m, 0)
                if conv:
                    conv_taps(c, even, range(4, TAPS))
                if fin:
                    pe.wait_ge(sum_ready, 3 * f + 3)
                    if moe:
                        pe.wait_ge(ct_ready, m + 1)
                    for b in range(PAIR):
                        last = pe.matmul(bank_b[b * D:b * D + D, 0:WIN], fold, total[:, b * WIN:(b + 1) * WIN],
                                         start=True, stop=True)
                    last.then_inc(fin_done, 1)
                if attn:
                    turn_p(n, 0)
                if moe:
                    hidden(m, even, 1)
                if attn:
                    turn_p(n, 1)
                if conv:
                    pe.wait_ge(h_ready, c + 1)
                    after(pe, out_ready, f + 1)
                    if moe:
                        pe.wait_ge(ct_ready, m + 1)
                    centre(c, 0, bank_b, h[even])
                if moe:
                    expert_out(m, 1)
                if attn:
                    pe.wait_ge(pt_ready[0], n + 1)
                    pe.wait_ge(pt_ready[1], n + 1)
                    for j in range(2):
                        for b in range(PAIR):
                            last = pe.matmul(bank_a[b * D:b * D + D, 0:WIN], v_sb[0:HALF, j, b * D:b * D + D],
                                             pt_sb[b][0:HALF, j, :], start=(j == 0), stop=(j == 1))
                    last.then_inc(pv_done, 1)
                if conv:
                    variance(c, 0, bank_b)
                if moe:
                    hidden(m, even, 2)
                if attn:
                    pe.wait_ge(h2_ready, n + 1)
                    centre(n, 1, bank_a, h2[odd])
                if moe:
                    expert_out(m, 2)
                if attn:
                    variance(n, 1, bank_a)
                if conv:
                    pe.wait_ge(xn_ready, c + 1)
                    pe.matmul(bank_b[:, 0:WIN], wq_sb[:, :], xn[:, :], start=True, stop=True).then_inc(q_done, 1)
                if moe:
                    hidden(m, even, 3)
                if conv:
                    if attn:
                        pe.wait_ge(pt_ready[0], n + 1)
                    pe.matmul(bank_s[0][:, 0:WIN], wk_sb[:, :], xn[:, :], start=True, stop=True)
                    for i in range(2):
                        at = WIN + i * VCOLS
                        last = pe.matmul(bank_s[0][0:HALF, at:at + VCOLS], xn[:, i * HALF:(i + 1) * HALF],
                                         wval[:, :], start=True, stop=True)
                    last.then_inc(kv_done, 1)
                if attn:
                    pe.wait_ge(xn2_ready, n + 1)
                    for i in range(2):
                        last = pe.matmul(bank_a[0:HALF, i * 16:i * 16 + 16], xn2[:, i * HALF:(i + 1) * HALF],
                                         wg_sb[:, :], start=True, stop=True)
                    last.then_inc(gate_done, 1)
                if moe:
                    expert_out(m, 3)

            run(pe, iteration)


def constants():
    half = np.arange(128) // D
    same = (half[:, None] == half[None, :]).astype(np.float32)
    sel = np.zeros((128, EPAIRS, 2, D), np.float32)
    for e in range(EXPERTS):
        sel[[e, EXPERTS + e], e // 2, e % 2, :] = 1.0
    return np.concatenate([np.eye(128, dtype=np.float32), np.eye(128, dtype=np.float32) - same / D, same / D,
                           np.tile(np.eye(D, dtype=np.float32), (2, 1)), sel.reshape(128, EPAIRS * 128)],
                          axis=1).astype(np.float32)


NAMES = ("x", "L0_tok_filt", "L0_tok_W_k", "L0_tok_b_k", "L0_attn_Wq", "L0_attn_bq", "L0_attn_Wk", "L0_attn_bk",
         "L0_attn_Wv", "L0_attn_bv", "L0_attn_Wo", "L0_attn_bo", "L0_ffn_Wg", "L0_ffn_bg", "L0_ffn_bias",
         "L0_ffn_W1", "L0_ffn_b1", "L0_ffn_W2", "L0_ffn_b2")


def kernel(x, L0_tok_filt, L0_tok_W_k, L0_tok_b_k, L0_attn_Wq, L0_attn_bq, L0_attn_Wk, L0_attn_bk, L0_attn_Wv,
           L0_attn_bv, L0_attn_Wo, L0_attn_bo, L0_ffn_Wg, L0_ffn_bg, L0_ffn_bias, L0_ffn_W1, L0_ffn_b1, L0_ffn_W2,
           L0_ffn_b2):
    import concourse.bacc as bacc
    from concourse.bass_utils import run_bass_kernel_spmd

    a = {k: np.asarray(v) for k, v in zip(NAMES, (
        x, L0_tok_filt, L0_tok_W_k, L0_tok_b_k, L0_attn_Wq, L0_attn_bq, L0_attn_Wk, L0_attn_bk, L0_attn_Wv,
        L0_attn_bv, L0_attn_Wo, L0_attn_bo, L0_ffn_Wg, L0_ffn_bg, L0_ffn_bias, L0_ffn_W1, L0_ffn_b1, L0_ffn_W2,
        L0_ffn_b2))}

    def diagonal(w):
        out = np.zeros((2 * D, 2 * w.shape[1]), w.dtype)
        out[0:D, 0:w.shape[1]] = w
        out[D:, w.shape[1]:] = w
        return out

    def twice(v):
        return np.concatenate([v, v]).reshape(128, 1)

    cols = np.concatenate([
        twice(a["L0_tok_b_k"]), twice(a["L0_attn_bq"]), twice(a["L0_attn_bk"]), twice(a["L0_attn_bo"]),
        a["L0_ffn_b1"].T, a["L0_ffn_b2"].reshape(EPAIRS, 128).T, a["L0_tok_filt"].T, twice(a["L0_attn_bv"])], axis=1)
    qk0 = [a["L0_attn_bq"][0:1]] * 2 + [a["L0_attn_bk"][0:1]] * 2
    rows = np.concatenate([a["L0_ffn_bg"]] * CHUNKS + [a["L0_ffn_bias"]] * CHUNKS + qk0
                          + [np.arange(EXPERTS, dtype=np.float32)] * CHUNKS)
    arrays = {
        "xt": a["x"].reshape(GROUPS, PAIR, LEN, DIN).transpose(0, 3, 1, 2),
        "wtok": a["L0_tok_W_k"].reshape(TAPS, DIN, D).transpose(1, 0, 2),
        "cols": cols,
        "rows": np.tile(rows, (128, 1)),
        "const": constants(),
        "bdq": diagonal(a["L0_attn_Wq"].T),
        "bdk": diagonal(a["L0_attn_Wk"].T),
        "wv": a["L0_attn_Wv"],
        "wot": a["L0_attn_Wo"].T,
        "bdg": diagonal(a["L0_ffn_Wg"]),
        "w1": a["L0_ffn_W1"].transpose(1, 0, 2),
        "w2": a["L0_ffn_W2"].transpose(1, 0, 2),
    }
    arrays = {k: np.ascontiguousarray(v) for k, v in arrays.items()}
    nc = bacc.Bacc("TRN2", target_bir_lowering=False, num_devices=1)
    aps = [nc.dram_tensor(k, v.shape, F32, kind="ExternalInput").ap() for k, v in arrays.items()]
    out = nc.dram_tensor("out", [GROUPS, 128, WIN], F32, kind="ExternalOutput").ap()
    audio_tower(nc, *aps, out)
    r = run_bass_kernel_spmd(nc, [arrays], core_ids=[0])
    return r.results[0]["out"].reshape(SEQS, D, WIN).transpose(0, 2, 1)
```

```python
from contextlib import ExitStack

import numpy as np
import concourse.bass as bass
from concourse import mybir

F32 = mybir.dt.float32
F32R = mybir.dt.float32r
U32 = mybir.dt.uint32
ALU = mybir.AluOpType
ACT = mybir.ActivationFunctionType
AX = mybir.AxisListType

SEQS, LEN, DIN = 32, 256, 128
TAPS, D = 8, 64
WIN = LEN - TAPS
HALF = WIN // 2
PAIR = 2
GROUPS = SEQS // PAIR
TOK = PAIR * WIN
EXPERTS, HID = 8, 128
EPAIRS = EXPERTS // 2
CHUNKS = 2 * PAIR
VCOLS = PAIR * D + 4
EPS = 1e-5
EXP_LN_SET = 6
KSCALE = D ** -0.5
HTAPS = TAPS // 2
SPAN = WIN + HTAPS

C_BTOK, C_BQ, C_BK, C_BO, C_B1, C_B2, C_FILT, C_BV = 0, 1, 2, 3, 4, 12, 16, 24
NCOLS = 25
R_BG, R_BIAS, R_QK0, R_IOTA = 0, 32, 64, 68
NROWS = 100
K_ID, K_CENTER, K_MEAN, K_FOLD = 0, 128, 256, 384
NCONST = K_FOLD + D


def audio_tower(nc, xt, wtok, cols, const, wqk, wv, wot, rows, bdg, w1, w2, out):
    ctx = ExitStack()
    with ctx:
        def sb(name, shape, dt=F32):
            return ctx.enter_context(nc.sbuf_tensor(name, shape, dt))

        def bank(name):
            return ctx.enter_context(nc.psum_tensor(name, [128, 512], F32))

        def sem(name):
            return ctx.enter_context(nc.semaphore(name))

        wtok_sb = sb("wtok_sb", [128, TAPS, D])
        wconv = sb("wconv", [128, HTAPS, 2, D])
        wconv_hi = sb("wconv_hi", [128, HTAPS, 2 * D], F32R)
        wconv_lo = sb("wconv_lo", [128, HTAPS, 2 * D], F32R)
        col = sb("col", [128, NCOLS])
        row = sb("row", [128, NROWS])
        cst = sb("cst", [128, NCONST])
        bqk = sb("bqk", [128, 1])
        eps = sb("eps", [128, 1])
        wqk_sb = sb("wqk_sb", [128, 2 * D])
        wqk_s = sb("wqk_s", [128, 2 * D])
        wqk_hi = sb("wqk_hi", [128, 2 * D], F32R)
        wqk_lo = sb("wqk_lo", [128, 2 * D], F32R)
        wv_sb = sb("wv_sb", [D, D])
        wot_sb = sb("wot_sb", [D, D])
        bv_wide = sb("bv_wide", [D, 128])
        wval = sb("wval", [128, VCOLS])
        bval = sb("bval", [128, VCOLS])
        wg_sb = sb("wg_sb", [128, 2 * EXPERTS])
        w1_sb = sb("w1_sb", [128, EXPERTS, HID])
        w1_hi = sb("w1_hi", [128, EXPERTS, HID], F32R)
        w1_lo = sb("w1_lo", [128, EXPERTS, HID], F32R)
        w2_sb = sb("w2_sb", [HID, EXPERTS, D])
        ident = cst[:, K_ID:K_ID + 128]
        center = cst[:, K_CENTER:K_CENTER + 128]
        meanof = cst[:, K_MEAN:K_MEAN + 128]
        fold = cst[:, K_FOLD:K_FOLD + D]

        x_sb = [sb(f"x{i}", [128, PAIR, LEN]) for i in range(2)]
        x_hi = sb("x_hi", [128, PAIR, LEN], F32R)
        x_lo = sb("x_lo", [128, PAIR, LEN], F32R)
        late = sb("late", [D, PAIR, WIN])
        hsum = sb("hsum", [128, WIN])
        h = [sb(f"h{i}", [128, WIN]) for i in range(2)]
        h2 = [sb(f"h2_{i}", [128, WIN]) for i in range(2)]
        sq = [sb(f"sq{i}", [128, WIN]) for i in range(2)]
        lnv = [sb(f"lnv{i}", [128, WIN]) for i in range(2)]
        rstd = [sb(f"rstd{i}", [128, WIN]) for i in range(2)]
        xn = sb("xn", [128, WIN])
        xn2 = sb("xn2", [128, WIN])
        ts = sb("ts", [128, TOK], F32R)
        xs = [sb(f"xs{i}", [128, TOK], F32R) for i in range(2)]
        qs = sb("qs", [128, TOK], F32R)
        kk = sb("kk", [128, 2, TOK], F32R)
        v_sb = sb("v_sb", [128, 2, VCOLS])
        kmask = sb("kmask", [128, 2, PAIR])
        mask = sb("mask", [128, 2, PAIR])
        nmax = sb("nmax", [128, PAIR, 2])
        psum_p = sb("psum_p", [128, PAIR, 2])
        rsum = sb("rsum", [128, PAIR, 2])
        rmask = sb("rmask", [128, PAIR, 2])
        p_sb = [sb(f"p{b}", [128, 2, WIN]) for b in range(PAIR)]
        pt_sb = [sb(f"pt{b}", [128, 2, WIN]) for b in range(PAIR)]
        lg = sb("lg", [128, CHUNKS, EXPERTS])
        top = sb("top", [128, CHUNKS, 8])
        topi = sb("topi", [128, CHUNKS, 8], U32)
        gbias = sb("gbias", [128, CHUNKS * EXPERTS])
        topf = sb("topf", [128, CHUNKS, 2])
        dlt = sb("dlt", [128, CHUNKS])
        eg = sb("eg", [128, CHUNKS])
        den = sb("den", [128, CHUNKS])
        gw1 = sb("gw1", [128, CHUNKS])
        gw2 = sb("gw2", [128, CHUNKS])
        oh1 = sb("oh1", [128, CHUNKS, EXPERTS])
        oh2 = sb("oh2", [128, CHUNKS, EXPERTS])
        cw1 = sb("cw1", [128, CHUNKS, EXPERTS])
        cw2 = sb("cw2", [128, CHUNKS, EXPERTS])
        cw = sb("cw", [128, CHUNKS, EXPERTS])
        ct_sb = sb("ct_sb", [EXPERTS, TOK])
        cb = sb("cb", [128, EPAIRS, TOK])
        hid = [sb(f"hid{i}", [128, TOK]) for i in range(4)]
        acc = [sb(f"acc{i}", [128, TOK]) for i in range(2)]
        total = sb("total", [128, TOK])

        bank_h = [bank("bank_h0"), bank("bank_h1")]
        bank_y = [bank("bank_y0"), bank("bank_y1")]
        bank_s = [bank("bank_s0"), bank("bank_s1")]
        bank_a = bank("bank_a")
        bank_b = bank("bank_b")

        par_conv = sem("par_conv")
        par_rest = sem("par_rest")
        set_pool = sem("set_pool")
        set_conv = sem("set_conv")
        set_dve = sem("set_dve")
        set_pe = sem("set_pe")
        passed = sem("passed")
        x_in = [sem("x_in0"), sem("x_in1")]
        o_out = [sem("o_out0"), sem("o_out1")]
        xh_ready = sem("xh_ready")
        xl_ready = sem("xl_ready")
        conv_done = sem("conv_done")
        late_ready = sem("late_ready")
        hsum_ready = sem("hsum_ready")
        h_ready = sem("h_ready")
        cen = [sem("cen1"), sem("cen2")]
        sqr = [sem("sqr1"), sem("sqr2")]
        var = [sem("var1"), sem("var2")]
        lnd = [sem("lnd1"), sem("lnd2")]
        rsd = [sem("rsd1"), sem("rsd2")]
        xn_ready = sem("xn_ready")
        xn2_ready = sem("xn2_ready")
        thi = sem("thi")
        tlo = sem("tlo")
        xhi = sem("xhi")
        xlo = sem("xlo")
        qk_done = sem("qk_done")
        qkh_ready = sem("qkh_ready")
        qkl_ready = sem("qkl_ready")
        k_copied = sem("k_copied")
        v_done = sem("v_done")
        v_ready = sem("v_ready")
        kmask_ready = sem("kmask_ready")
        mask_ready = sem("mask_ready")
        sc_done = sem("sc_done")
        nmax_ready = sem("nmax_ready")
        ex_ready = sem("ex_ready")
        rs_ready = sem("rs_ready")
        rm_ready = sem("rm_ready")
        p_ready = sem("p_ready")
        pt_done = sem("pt_done")
        pt_ready = sem("pt_ready")
        pv_done = sem("pv_done")
        h2_ready = sem("h2_ready")
        gate_done = sem("gate_done")
        topk = sem("topk")
        dlt_ready = sem("dlt_ready")
        eg_ready = sem("eg_ready")
        ct_done = sem("ct_done")
        ct_ready = sem("ct_ready")
        cb_in = [sem(f"cb_in{p}") for p in range(EPAIRS)]
        l1_done = sem("l1_done")
        hid_ready = [sem("hid_even"), sem("hid_odd")]
        y_done = sem("y_done")
        acc_ready = sem("acc_ready")
        sum_ready = sem("sum_ready")
        fin_done = sem("fin_done")
        out_ready = sem("out_ready")

        N_CONV, N_REST = 2, 10
        TOPK = 10

        def after(eng, s, value):
            if not isinstance(value, int) or value > 0:
                eng.wait_ge(s, value)

        def hold(eng, s, value):
            eng.wait_ge(s, value)
            eng.sem_inc(passed, 1)

        def after_hold(eng, s, value):
            if not isinstance(value, int) or value > 0:
                hold(eng, s, value)

        def run(iteration, eng):
            iteration(-2, 0, True, False, False, False, False)
            iteration(-1, 1, True, True, False, False, False)
            iteration(0, 0, True, True, True, False, False)
            iteration(1, 1, True, True, True, True, False)
            with eng.Fori(0, (GROUPS - 4) // 2) as i:
                iteration(i * 2 + 2, 0, True, True, True, True, True)
                iteration(i * 2 + 3, 1, True, True, True, True, True)
            iteration(GROUPS - 2, 0, False, True, True, True, True)
            iteration(GROUPS - 1, 1, False, False, True, True, True)
            iteration(GROUPS, 0, False, False, False, True, True)
            iteration(GROUPS + 1, 1, False, False, False, False, True)

        block = ctx.enter_context(nc.Block())

        @block.sync
        def _(sp):
            sp.dma_start(wtok_sb[:, :, :], wtok).then_inc(par_conv, 16)

            sp.dma_start(x_sb[0][:, :, :], xt[0]).then_inc(x_in[0], 16)
            for dst, src in ((cst[:, :], const), (wv_sb[:, :], wv), (w1_sb[0:D, :, :], w1),
                             (row[:, :], rows), (w2_sb[:, :, :], w2)):
                sp.dma_start(dst, src).then_inc(par_rest, 16)

            def spread(m, p):
                if p == 0:
                    hold(sp, ct_ready, m + 1)
                    after_hold(sp, acc_ready, 4 * m)
                for s in range(2):
                    e = 2 * p + s
                    sp.dma_start(cb[s * D:s * D + D, p, :],
                                 ct_sb[e:e + 1, :].unsqueeze(1).to_broadcast([1, D, TOK])).then_inc(cb_in[p], 16)

            def iteration(t, odd, d_, c_, n_, m_, f_):
                d, c, m, f = t + 2, t + 1, t - 1, t - 2
                if m_:
                    spread(m, 0)
                    spread(m, 1)
                if f_:
                    hold(sp, out_ready, f + 1)
                    sp.dma_start(out[f], h2[odd][:, :]).then_inc(o_out[odd], 16)
                if d_:
                    after_hold(sp, xh_ready, d - 1)
                    after_hold(sp, xl_ready, d - 1)
                    if not (isinstance(t, int) and d == 0):
                        sp.dma_start(x_sb[odd][:, :, :], xt[d]).then_inc(x_in[odd], 16)
                if m_:
                    spread(m, 2)
                    spread(m, 3)
                if c_:
                    hold(sp, qkl_ready, 2 * c + 2)
                    sp.dma_start(kk[0:D, :, :].bitcast(F32), kk[D:128, :, :].bitcast(F32)).then_inc(k_copied, 16)

            run(iteration, sp)
            for i in range(2):
                sp.wait_ge(o_out[i], 16 * GROUPS // 2)

        @block.gpsimd
        def _(pool):
            pool.memset(eps[:, :], EPS).then_inc(set_pool, 1)

            def scale(n, b):
                pool.wait_ge(rm_ready, 2 * n + b + 1)
                pool.tensor_tensor(p_sb[b][0:HALF, :, :], p_sb[b][0:HALF, :, :],
                                   rmask[0:HALF, b, :].unsqueeze(2).to_broadcast([HALF, 2, WIN]),
                                   ALU.mult).then_inc(p_ready, 1)

            def add(m, p):
                pool.wait_ge(acc_ready, 4 * m + p + 1)
                if p == 1:
                    after(pool, fin_done, m)
                    pool.tensor_tensor(total[:, :], acc[0][:, :], acc[1][:, :], ALU.add).then_inc(sum_ready, 1)
                else:
                    pool.wait_ge(sum_ready, 3 * m + p - 1)
                    pool.tensor_tensor(total[:, :], total[:, :], acc[p % 2][:, :], ALU.add).then_inc(sum_ready, 1)

            def iteration(t, odd, d_, c_, n_, m_, f_):
                d, c, n, m = t + 2, t + 1, t, t - 1
                if n_:
                    scale(n, 1)
                if m_:
                    add(m, 1)
                if d_:
                    pool.wait_ge(xh_ready, d + 1)
                    pool.tensor_tensor(x_lo[:, :, :], x_sb[odd][:, :, :], x_hi[:, :, :].bitcast(F32),
                                       ALU.subtract).then_inc(xl_ready, 1)
                if m_:
                    add(m, 2)
                    add(m, 3)
                if c_:
                    scale(c, 0)

            run(iteration, pool)

        @block.scalar
        def _(act):
            act.add_instruction(mybir.InstLoadActFuncSet(
                name=nc.get_next_instruction_name(), engine=mybir.EngineType.Activation, ins=[], outs=[],
                act_func_set_id=EXP_LN_SET))
            act.dma_start(col[:, :], cols).then_inc(par_conv, 16)
            for dst, src in ((wqk_sb[0:D, :], wqk), (wqk_sb[D:128, :], wqk), (wot_sb[:, :], wot),
                             (w1_sb[D:128, :, :], w1), (wg_sb[:, :], bdg)):
                act.dma_start(dst, src).then_inc(par_rest, 16)

            def exps(n, b):
                act.wait_ge(nmax_ready, 2 * n + b + 1)
                after(act, pt_done, 2 * n + b - 1)
                after(act, rs_ready, 2 * n + b - 1)
                for i in range(2):
                    last = act.activation(p_sb[b][0:HALF, i, :], bank_s[b][0:HALF, i * WIN:(i + 1) * WIN], ACT.Exp,
                                          bias=nmax[0:HALF, b, i:i + 1], accum_out=psum_p[0:HALF, b, i:i + 1])
                last.then_inc(ex_ready, 1)

            def relu(m, e):
                p, s = e // 2, e % 2
                act.wait_ge(l1_done, 8 * m + e + 1)
                after(act, y_done, 4 * m + p - 1)
                act.activation(hid[2 * (p % 2) + s][:, :], bank_h[s][:, 0:TOK], ACT.Relu,
                               bias=col[:, C_B1 + e:C_B1 + e + 1]).then_inc(hid_ready[s], 1)

            def square(g, which, src):
                act.wait_ge(cen[which], g + 1)
                after(act, var[which], g)
                act.activation(sq[which][:, :], src[:, 0:WIN], ACT.Square).then_inc(sqr[which], 1)

            def rsqrt(g, which, src, used):
                act.wait_ge(var[which], g + 1)
                act.activation(lnv[which][:, :], src[:, WIN:2 * WIN], ACT.Ln, bias=eps[:, :]).then_inc(lnd[which], 1)
                act.wait_ge(lnd[which], g + 1)
                after(act, used, g)
                act.activation(rstd[which][:, :], lnv[which][:, :], ACT.Exp, scale=-0.5).then_inc(rsd[which], 1)

            def high_parts(dst, src):
                act.activation(dst[0:D, 0:WIN], src[0:D, :], ACT.Copy)
                return act.activation(dst[D:128, WIN:TOK], src[D:128, :], ACT.Copy)

            def turned(n, b):
                act.wait_ge(pt_done, 2 * n + b + 1)
                after(act, pv_done, n)
                act.activation(pt_sb[b][0:HALF, :, :], bank_s[b][0:HALF, 0:TOK].rearrange("p (a b) -> p a b", a=2),
                               ACT.Copy).then_inc(pt_ready, 1)

            def later_taps(c):
                act.wait_ge(conv_done, c + 1)
                after(act, hsum_ready, c)
                act.activation(late[:, :, :],
                               bank_a[D:128, 0:PAIR * SPAN].rearrange("p (a b) -> p a b", a=PAIR)[:, :, HTAPS:SPAN],
                               ACT.Identity, bias=col[D:128, C_BTOK:C_BTOK + 1]).then_inc(late_ready, 1)

            def high_queries_keys(c):
                act.wait_ge(qk_done, c + 1)
                after(act, sc_done, 2 * c)
                act.activation(qs[0:D, :], bank_b[0:D, 0:TOK], ACT.Identity, bias=bqk[0:D, :])
                act.activation(kk[D:128, 0, :], bank_b[D:128, 0:TOK], ACT.Identity,
                               bias=bqk[D:128, :]).then_inc(qkh_ready, 1)

            act.wait_ge(par_conv, 16 * N_CONV)
            act.wait_ge(set_pool, 1)

            def iteration(t, odd, d_, c_, n_, m_, f_):
                d, c, n, m = t + 2, t + 1, t, t - 1
                even = 1 - odd
                if m_:
                    relu(m, 2)
                if n_:
                    exps(n, 0)
                if m_:
                    relu(m, 3)
                if n_:
                    exps(n, 1)
                if m_:
                    relu(m, 4)
                if c_:
                    act.wait_ge(hsum_ready, c + 1)
                    after(act, h2_ready, c - 1)
                    act.activation(h[even][:, :], hsum[:, :], ACT.Relu).then_inc(h_ready, 1)
                if n_:
                    turned(n, 0)
                if c_:
                    square(c, 0, bank_b)
                if n_:
                    turned(n, 1)
                if c_:
                    rsqrt(c, 0, bank_b, xn_ready)
                if m_:
                    relu(m, 5)
                if c_:
                    act.wait_ge(xn_ready, c + 1)
                    after(act, qk_done, c)
                    high_parts(ts, xn).then_inc(thi, 1)
                if m_:
                    relu(m, 6)
                if d_:
                    act.wait_ge(x_in[odd], 8 * (d - odd) + 16)
                    after(act, conv_done, d)
                    act.activation(x_hi[:, :, :], x_sb[odd][:, :, :], ACT.Copy).then_inc(xh_ready, 1)
                if n_:
                    square(n, 1, bank_s[0])
                if c_:
                    high_queries_keys(c)
                if n_:
                    rsqrt(n, 1, bank_s[0], xn2_ready)
                    act.wait_ge(xn2_ready, n + 1)
                    after(act, l1_done, 8 * (n - 1))
                    high_parts(xs[odd], xn2).then_inc(xhi, 1)
                    act.wait_ge(dlt_ready, n + 1)
                    act.activation(eg[0:HALF, :], dlt[0:HALF, :], ACT.Exp).then_inc(eg_ready, 1)
                    relu(n, 0)
                    relu(n, 1)
                if d_:
                    later_taps(d)

            run(iteration, act)

        @block.vector
        def _(dve):
            dve.wait_ge(par_conv, 16 * N_CONV)
            dve.tensor_tensor(wconv[:, :, :, :], wtok_sb[:, :, :].rearrange("p (s f) k -> p f s k", s=2),
                              col[:, C_FILT:C_FILT + TAPS].rearrange("p (s f) -> p f s", s=2).unsqueeze(3)
                              .to_broadcast([128, HTAPS, 2, D]), ALU.mult).then_inc(set_conv, 1)
            dve.wait_ge(set_conv, 1)
            wide_w = wconv[:, :, :, :].rearrange("p f s k -> p f (s k)")
            dve.tensor_copy(wconv_hi[:, :, :], wide_w).then_inc(set_conv, 1)
            dve.wait_ge(set_conv, 2)
            dve.tensor_tensor(wconv_lo[:, :, :], wide_w, wconv_hi[:, :, :].bitcast(F32),
                              ALU.subtract).then_inc(set_conv, 1)
            dve.wait_ge(par_rest, 16 * N_REST)
            dve.tensor_copy(bqk[0:D, :], col[0:D, C_BQ:C_BQ + 1])
            dve.tensor_scalar(bqk[D:128, :], col[D:128, C_BK:C_BK + 1], KSCALE, None, ALU.mult)
            dve.tensor_copy(bv_wide[:, :], col[0:D, C_BV:C_BV + 1].to_broadcast([D, 128]))
            dve.tensor_copy(wqk_s[:, 0:D], wqk_sb[:, 0:D])
            dve.tensor_scalar(wqk_s[:, D:], wqk_sb[:, D:], KSCALE, None, ALU.mult).then_inc(set_dve, 1)
            dve.wait_ge(set_dve, 1)
            dve.tensor_copy(wqk_hi[:, :], wqk_s[:, :])
            dve.memset(wval[:, :], 0.0)
            dve.tensor_copy(w1_hi[:, :, :], w1_sb[:, :, :]).then_inc(set_dve, 1)
            dve.wait_ge(set_dve, 2)
            dve.tensor_tensor(wqk_lo[:, :], wqk_s[:, :], wqk_hi[:, :].bitcast(F32), ALU.subtract)
            for j in range(2):
                rows_j = slice(j * D, j * D + D)
                dve.tensor_copy(wval[rows_j, 128 + j:129 + j], wqk_sb[rows_j, 0:1])
                dve.tensor_copy(wval[rows_j, 130 + j:131 + j], wqk_sb[rows_j, D:D + 1])
            dve.tensor_tensor(gbias[:, :], row[:, R_BG:R_BG + 32], row[:, R_BIAS:R_BIAS + 32], ALU.add)
            dve.tensor_copy(bval[:, PAIR * D:VCOLS], row[:, R_QK0:R_QK0 + 4]).then_inc(set_dve, 1)

            def value_weights():
                dve.wait_ge(set_pe, 1)
                for b in range(PAIR):
                    rows_b = slice(b * D, b * D + D)
                    dve.tensor_copy(wval[rows_b, b * D:b * D + D], bank_y[0][rows_b, 0:D])
                    last = dve.tensor_copy(bval[:, b * D:b * D + D], bank_y[0][:, D:2 * D])
                last.then_inc(set_dve, 1)
                dve.tensor_tensor(w1_lo[:, :, :], w1_sb[:, :, :], w1_hi[:, :, :].bitcast(F32),
                                  ALU.subtract).then_inc(set_dve, 1)

            def relu(m, e):
                p, s = e // 2, e % 2
                dve.wait_ge(l1_done, 8 * m + e + 1)
                after(dve, y_done, 4 * m + p - 1)
                dve.tensor_scalar(hid[2 * (p % 2) + s][:, :], bank_h[s][:, 0:TOK],
                                  col[:, C_B1 + e:C_B1 + e + 1], 0.0, ALU.add, ALU.max).then_inc(hid_ready[s], 1)

            def weigh(m, p):
                dve.wait_ge(y_done, 4 * m + p + 1)
                dve.wait_ge(cb_in[p], 32 * m + 32)
                after(dve, sum_ready, 3 * m + (-1, 0, 1, 1)[p])
                dve.scalar_tensor_tensor(out=acc[p % 2][:, :], in0=bank_y[p % 2][:, 0:TOK],
                                         scalar=col[:, C_B2 + p:C_B2 + p + 1], in1=cb[:, p, :], op0=ALU.add,
                                         op1=ALU.mult).then_inc(acc_ready, 1)

            def rowmax(n, b):
                dve.wait_ge(sc_done, 2 * n + b + 1)
                after(dve, ex_ready, 2 * n + b - 1)
                dve.tensor_reduce(nmax[0:HALF, b, :], bank_s[b][0:HALF, 0:TOK].rearrange("p (a b) -> p a b", a=2),
                                  AX.X, ALU.max, negate=True).then_inc(nmax_ready, 1)

            def recip(n, b):
                dve.wait_ge(ex_ready, 2 * n + b + 1)
                after(dve, p_ready, 2 * n + b - 1)
                dve.reciprocal(rsum[0:HALF, b, :], psum_p[0:HALF, b, :]).then_inc(rs_ready, 1)
                dve.wait_ge(rs_ready, 2 * n + b + 1)
                dve.wait_ge(mask_ready, n + 1)
                dve.tensor_tensor(rmask[0:HALF, b, :], rsum[0:HALF, b, :], mask[0:HALF, :, b],
                                  ALU.mult).then_inc(rm_ready, 1)

            def low_parts(dst, src):
                dve.tensor_tensor(dst[D:128, 0:WIN], src[0:D, :], dst[0:D, 0:WIN].bitcast(F32), ALU.subtract)
                return dve.tensor_tensor(dst[0:D, WIN:TOK], src[D:128, :], dst[D:128, WIN:TOK].bitcast(F32),
                                         ALU.subtract)

            T = slice(0, HALF)

            def by_chunk(a):
                return a.rearrange("p (a b) -> p a b", a=CHUNKS)

            def wide(a):
                return a.unsqueeze(2).to_broadcast([HALF, CHUNKS, EXPERTS])

            def seen(m, k):
                dve.wait_ge(topk, TOPK * m + k)

            def logits(m):
                dve.wait_ge(gate_done, m + 1)
                dve.tensor_tensor(lg[T, :, :], by_chunk(bank_s[0][T, 0:CHUNKS * EXPERTS]), by_chunk(gbias[T, :]),
                                  ALU.add).then_inc(topk, 1)

            def largest(m):
                hold(dve, topk, TOPK * m + 1)
                for j in range(CHUNKS):
                    last = dve.max(top[T, j, :], lg[T, j, :])
                last.then_inc(topk, 1)

            def difference(m):
                seen(m, 2)
                dve.tensor_tensor(dlt[T, :], top[T, :, 1], top[T, :, 0], ALU.subtract).then_inc(dlt_ready, 1)

            def indices(m):
                for j in range(CHUNKS):
                    last = dve.max_index(topi[T, j, :], top[T, j, :], lg[T, j, :])
                last.then_inc(topk, 1)

            def denominator(m):
                seen(m, 3)
                dve.tensor_copy(topf[T, :, :], topi[T, :, 0:2]).then_inc(topk, 1)
                dve.wait_ge(eg_ready, m + 1)
                dve.tensor_scalar(den[T, :], eg[T, :], 1.0, None, ALU.add).then_inc(topk, 1)

            def one_hot(m):
                iota = by_chunk(row[T, R_IOTA:R_IOTA + 32])
                seen(m, 5)
                dve.reciprocal(gw1[T, :], den[T, :]).then_inc(topk, 1)
                dve.tensor_tensor(oh1[T, :, :], iota, wide(topf[T, :, 0]), ALU.is_equal)
                dve.tensor_tensor(oh2[T, :, :], iota, wide(topf[T, :, 1]), ALU.is_equal).then_inc(topk, 1)

            def weights(m):
                seen(m, 6)
                dve.tensor_tensor(gw2[T, :], eg[T, :], gw1[T, :], ALU.mult).then_inc(topk, 1)
                seen(m, 7)
                dve.tensor_tensor(cw1[T, :, :], oh1[T, :, :], wide(gw1[T, :]), ALU.mult)

            def second_weight(m):
                seen(m, 8)
                dve.tensor_tensor(cw2[T, :, :], oh2[T, :, :], wide(gw2[T, :]), ALU.mult).then_inc(topk, 1)

            def both_weights(m):
                seen(m, 9)
                after(dve, ct_done, m)
                dve.tensor_tensor(cw[T, :, :], cw1[T, :, :], cw2[T, :, :], ALU.add).then_inc(topk, 1)

            def both_taps(c):
                dve.wait_ge(late_ready, c + 1)
                after(dve, h_ready, c)
                for b in range(PAIR):
                    last = dve.tensor_tensor(hsum[b * D:b * D + D, :], bank_a[0:D, b * SPAN:b * SPAN + WIN],
                                             late[:, b, :], ALU.add)
                last.then_inc(hsum_ready, 1)

            def keep_weights(m):
                dve.wait_ge(ct_done, m + 1)
                for p in range(EPAIRS):
                    after(dve, cb_in[p], 32 * m)
                dve.tensor_copy(ct_sb[:, :], bank_b[0:EXPERTS, 0:TOK]).then_inc(ct_ready, 1)

            def normalise(c):
                dve.wait_ge(rsd[0], c + 1)
                after(dve, v_done, c)
                after(dve, tlo, c)
                dve.tensor_tensor(xn[:, :], bank_b[:, 0:WIN], rstd[0][:, :], ALU.mult).then_inc(xn_ready, 1)

            def normalise_2(n):
                dve.wait_ge(rsd[1], n + 1)
                after(dve, gate_done, n)
                after(dve, xlo, n)
                dve.tensor_tensor(xn2[:, :], bank_s[0][:, 0:WIN], rstd[1][:, :], ALU.mult).then_inc(xn2_ready, 1)

            def keep_values(c):
                dve.wait_ge(v_done, c + 1)
                after(dve, pv_done, c)
                dve.tensor_tensor(v_sb[0:HALF, :, :],
                                  bank_s[1][0:HALF, 0:2 * VCOLS].rearrange("p (a b) -> p a b", a=2),
                                  bval[0:HALF, :].unsqueeze(1).to_broadcast([HALF, 2, VCOLS]),
                                  ALU.add).then_inc(v_ready, 1)

            def low_queries(c):
                dve.wait_ge(qkh_ready, c + 1)
                dve.scalar_tensor_tensor(out=qs[D:128, :], in0=bank_b[0:D, 0:TOK], scalar=bqk[0:D, :],
                                         in1=qs[0:D, :].bitcast(F32), op0=ALU.add,
                                         op1=ALU.subtract).then_inc(qkl_ready, 1)

            def low_keys(c):
                dve.wait_ge(qkh_ready, c + 1)
                dve.scalar_tensor_tensor(out=kk[D:128, 1, :], in0=bank_b[D:128, 0:TOK], scalar=bqk[D:128, :],
                                         in1=kk[D:128, 0, :].bitcast(F32), op0=ALU.add,
                                         op1=ALU.subtract).then_inc(qkl_ready, 1)

            def masks(c):
                dve.wait_ge(v_ready, c + 1)
                dve.tensor_scalar(kmask[0:HALF, :, :], v_sb[0:HALF, :, 130:132], 0.0, None,
                                  ALU.not_equal).then_inc(kmask_ready, 1)
                dve.wait_ge(kmask_ready, c + 1)
                dve.scalar_tensor_tensor(out=mask[0:HALF, :, :], in0=v_sb[0:HALF, :, 128:130], scalar=0.0,
                                         in1=kmask[0:HALF, :, :], op0=ALU.not_equal,
                                         op1=ALU.mult).then_inc(mask_ready, 1)

            def iteration(t, odd, d_, c_, n_, m_, f_):
                c, n, m, f = t + 1, t, t - 1, t - 2
                if m_:
                    both_weights(m)
                if n_:
                    rowmax(n, 0)
                if f_:
                    weigh(f, 3)
                if m_:
                    keep_weights(m)
                if n_:
                    rowmax(n, 1)
                    recip(n, 0)
                if c_:
                    both_taps(c)
                if n_:
                    recip(n, 1)
                if f_:
                    dve.wait_ge(fin_done, f + 1)
                    dve.tensor_tensor(h2[odd][:, :], bank_b[:, 0:WIN], h2[odd][:, :], ALU.add).then_inc(out_ready, 1)
                if m_:
                    weigh(m, 0)
                    weigh(m, 1)
                if c_:
                    if isinstance(t, int) and c == 0:
                        value_weights()
                    normalise(c)
                if n_:
                    dve.wait_ge(pv_done, n + 1)
                    after(dve, o_out[odd], 8 * (n - odd))
                    dve.scalar_tensor_tensor(out=h2[odd][:, :], in0=bank_s[0][:, 0:WIN], scalar=col[:, C_BO:C_BO + 1],
                                             in1=h[odd][:, :], op0=ALU.add, op1=ALU.add).then_inc(h2_ready, 1)
                if c_:
                    dve.wait_ge(thi, c + 1)
                    low_parts(ts, xn).then_inc(tlo, 1)
                if m_:
                    weigh(m, 2)
                    relu(m, 7)
                if c_:
                    low_queries(c)
                if n_:
                    normalise_2(n)
                if c_:
                    low_keys(c)
                    keep_values(c)
                if n_:
                    logits(n)
                    dve.wait_ge(xhi, n + 1)
                    low_parts(xs[odd], xn2).then_inc(xlo, 1)
                    largest(n)
                    difference(n)
                    indices(n)
                    denominator(n)
                    one_hot(n)
                if c_:
                    masks(c)
                if n_:
                    weights(n)
                    second_weight(n)

            run(iteration, dve)

        @block.tensor
        def _(pe):
            def conv(c, steps):
                passes = [(w, x, j) for w, x in ((wconv_hi, x_hi), (wconv_hi, x_lo), (wconv_lo, x_hi))
                          for j in range(HTAPS)]
                if 0 in steps:
                    pe.wait_ge(xh_ready, c + 1)
                    pe.wait_ge(xl_ready, c + 1)
                    after(pe, hsum_ready, c)
                for k in steps:
                    w, x, j = passes[k]
                    last = pe.matmul(bank_a[:, 0:PAIR * SPAN].rearrange("p (a b) -> p a b", a=PAIR), w[:, j, :],
                                     x[:, :, j:j + SPAN], start=(k == 0), stop=(k == len(passes) - 1))
                if len(passes) - 1 in steps:
                    last.then_inc(conv_done, 1)

            def scores(n, b):
                pe.wait_ge(k_copied, 16 * n + 16)
                pe.wait_ge(qkl_ready, 2 * n + 2)
                if b == 0:
                    after(pe, topk, TOPK * (n - 1) + 1)
                else:
                    pe.wait_ge(v_ready, n + 1)
                for i in range(2):
                    for part in range(2):
                        last = pe.matmul(bank_s[b][0:HALF, i * WIN:(i + 1) * WIN],
                                         qs[:, b * WIN + i * HALF:b * WIN + (i + 1) * HALF],
                                         kk[:, part, b * WIN:(b + 1) * WIN], start=(part == 0), stop=(part == 1))
                last.then_inc(sc_done, 1)

            def turn_p(n, b):
                pe.wait_ge(p_ready, 2 * n + b + 1)
                for j in range(2):
                    for i in range(2):
                        at = j * WIN + i * HALF
                        last = pe.transpose(bank_s[b][0:HALF, at:at + HALF],
                                            p_sb[b][0:HALF, i, j * HALF:(j + 1) * HALF], ident[0:HALF, 0:HALF])
                last.then_inc(pt_done, 1)

            def turn_weights(m):
                pe.wait_ge(topk, TOPK * m + TOPK)
                if isinstance(m, int) and m == GROUPS - 1:
                    pe.wait_ge(out_ready, m - 1)
                else:
                    pe.wait_ge(qkl_ready, 2 * m + 4)
                for j in range(CHUNKS):
                    i, b = j // PAIR, j % PAIR
                    at = b * WIN + i * HALF
                    last = pe.transpose(bank_b[0:EXPERTS, at:at + HALF], cw[0:HALF, j, :], ident[0:HALF, 0:HALF])
                last.then_inc(ct_done, 1)

            def hidden(m, par, e):
                if e == 0:
                    if isinstance(m, int) and m == 0:
                        pe.wait_ge(set_dve, 5)
                    pe.wait_ge(xhi, m + 1)
                    pe.wait_ge(xlo, m + 1)
                after(pe, hid_ready[e % 2], 4 * m + e // 2)
                pe.matmul(bank_h[e % 2][:, 0:TOK], w1_hi[:, e, :], xs[par][:, :], start=True, stop=False)
                pe.matmul(bank_h[e % 2][:, 0:TOK], w1_lo[:, e, :], xs[par][:, :], start=False,
                          stop=True).then_inc(l1_done, 1)

            def expert_out(m, p):
                pe.wait_ge(hid_ready[0], 4 * m + p + 1)
                pe.wait_ge(hid_ready[1], 4 * m + p + 1)
                after(pe, acc_ready, 4 * m + p - 1)
                for s in range(2):
                    last = pe.matmul(bank_y[p % 2][s * D:s * D + D, 0:TOK], w2_sb[:, 2 * p + s, :],
                                     hid[2 * (p % 2) + s][:, :], start=True, stop=True)
                last.then_inc(y_done, 1)

            def centre(g, which, dst, src):
                pe.matmul(dst[:, 0:WIN], center, src[:, :], start=True, stop=True).then_inc(cen[which], 1)

            def variance(g, which, dst):
                pe.wait_ge(sqr[which], g + 1)
                pe.matmul(dst[:, WIN:2 * WIN], meanof, sq[which][:, :], start=True, stop=True).then_inc(var[which], 1)

            def parameter_products():
                pe.wait_ge(par_rest, 16 * N_REST)
                pe.wait_ge(set_dve, 3)
                for b in range(PAIR):
                    pe.matmul(bank_y[0][b * D:b * D + D, 0:D], wv_sb[:, :], wot_sb[:, :], start=True, stop=True)
                pe.matmul(bank_y[0][:, D:2 * D], bv_wide[:, :], wot_sb[:, :], start=True, stop=True).then_inc(set_pe, 1)

            pe.wait_ge(set_conv, 3)

            def fold_halves(f):
                pe.wait_ge(sum_ready, 3 * f + 3)
                if isinstance(f, int) and f == GROUPS - 1:
                    pe.wait_ge(out_ready, f)
                else:
                    pe.wait_ge(ct_ready, f + 2)
                for b in range(PAIR):
                    last = pe.matmul(bank_b[b * D:b * D + D, 0:WIN], fold, total[:, b * WIN:(b + 1) * WIN],
                                     start=True, stop=True)
                last.then_inc(fin_done, 1)

            def first_centre(c, par):
                pe.wait_ge(h_ready, c + 1)
                if isinstance(c, int) and c < 3:
                    after(pe, qkl_ready, 2 * c)
                    after(pe, ct_ready, c - 1)
                else:
                    pe.wait_ge(out_ready, c - 2)
                centre(c, 0, bank_b, h[par])

            def attend(n):
                pe.wait_ge(pt_ready, 2 * n + 2)
                for j in range(2):
                    for b in range(PAIR):
                        last = pe.matmul(bank_s[0][b * D:b * D + D, 0:WIN], v_sb[0:HALF, j, b * D:b * D + D],
                                         pt_sb[b][0:HALF, j, :], start=(j == 0), stop=(j == 1))
                last.then_inc(pv_done, 1)

            def queries_keys(c):
                pe.wait_ge(thi, c + 1)
                pe.wait_ge(tlo, c + 1)
                pe.matmul(bank_b[:, 0:TOK], wqk_hi[:, :], ts[:, :], start=True, stop=False)
                pe.matmul(bank_b[:, 0:TOK], wqk_lo[:, :], ts[:, :], start=False, stop=True).then_inc(qk_done, 1)

            def values(c):
                if isinstance(c, int) and c == 0:
                    pe.wait_ge(set_dve, 4)
                pe.wait_ge(xn_ready, c + 1)
                after(pe, pt_ready, 2 * c)
                for i in range(2):
                    last = pe.matmul(bank_s[1][0:HALF, i * VCOLS:(i + 1) * VCOLS], xn[:, i * HALF:(i + 1) * HALF],
                                     wval[:, :], start=True, stop=True)
                last.then_inc(v_done, 1)

            def iteration(t, odd, d_, c_, n_, m_, f_):
                c, n, m, f = t + 1, t, t - 1, t - 2
                even = 1 - odd
                if m_:
                    pe.wait_ge(h2_ready, m + 1)
                    centre(m, 1, bank_s[0], h2[even])
                if n_:
                    queries_keys(n)
                if f_:
                    hidden(f, odd, 7)
                if m_:
                    variance(m, 1, bank_s[0])
                if n_:
                    values(n)
                if c_:
                    conv(c, range(0, 8))
                if m_:
                    pe.wait_ge(xn2_ready, m + 1)
                    for i in range(2):
                        last = pe.matmul(bank_s[0][0:HALF, i * 16:i * 16 + 16], xn2[:, i * HALF:(i + 1) * HALF],
                                         wg_sb[:, :], start=True, stop=True)
                    last.then_inc(gate_done, 1)
                if c_:
                    conv(c, range(8, 10))
                if f_:
                    expert_out(f, 3)
                if m_:
                    hidden(m, even, 0)
                    hidden(m, even, 1)
                if c_:
                    conv(c, range(10, 12))
                if n_:
                    scores(n, 0)
                if m_:
                    hidden(m, even, 2)
                    hidden(m, even, 3)
                    turn_weights(m)
                if n_:
                    scores(n, 1)
                if m_:
                    expert_out(m, 0)
                    hidden(m, even, 4)
                if f_:
                    fold_halves(f)
                if m_:
                    expert_out(m, 1)
                if n_:
                    turn_p(n, 0)
                if c_:
                    if isinstance(t, int) and c == 0:
                        parameter_products()
                    first_centre(c, even)
                if n_:
                    turn_p(n, 1)
                if c_:
                    variance(c, 0, bank_b)
                if m_:
                    hidden(m, even, 5)
                if n_:
                    attend(n)
                if m_:
                    hidden(m, even, 6)
                    expert_out(m, 2)

            run(iteration, pe)


def constants():
    half = np.arange(128) // D
    same = (half[:, None] == half[None, :]).astype(np.float32)
    eye = np.eye(128, dtype=np.float32)
    return np.concatenate([eye, eye - same / D, same / D, np.tile(np.eye(D, dtype=np.float32), (2, 1))],
                          axis=1).astype(np.float32)


NAMES = ("x", "L0_tok_filt", "L0_tok_W_k", "L0_tok_b_k", "L0_attn_Wq", "L0_attn_bq", "L0_attn_Wk", "L0_attn_bk",
         "L0_attn_Wv", "L0_attn_bv", "L0_attn_Wo", "L0_attn_bo", "L0_ffn_Wg", "L0_ffn_bg", "L0_ffn_bias",
         "L0_ffn_W1", "L0_ffn_b1", "L0_ffn_W2", "L0_ffn_b2")


def kernel(x, L0_tok_filt, L0_tok_W_k, L0_tok_b_k, L0_attn_Wq, L0_attn_bq, L0_attn_Wk, L0_attn_bk, L0_attn_Wv,
           L0_attn_bv, L0_attn_Wo, L0_attn_bo, L0_ffn_Wg, L0_ffn_bg, L0_ffn_bias, L0_ffn_W1, L0_ffn_b1, L0_ffn_W2,
           L0_ffn_b2):
    import concourse.bacc as bacc
    from concourse.bass_utils import run_bass_kernel_spmd

    a = {k: np.asarray(v) for k, v in zip(NAMES, (
        x, L0_tok_filt, L0_tok_W_k, L0_tok_b_k, L0_attn_Wq, L0_attn_bq, L0_attn_Wk, L0_attn_bk, L0_attn_Wv,
        L0_attn_bv, L0_attn_Wo, L0_attn_bo, L0_ffn_Wg, L0_ffn_bg, L0_ffn_bias, L0_ffn_W1, L0_ffn_b1, L0_ffn_W2,
        L0_ffn_b2))}

    def diagonal(w):
        out = np.zeros((2 * D, 2 * w.shape[1]), w.dtype)
        out[0:D, 0:w.shape[1]] = w
        out[D:, w.shape[1]:] = w
        return out

    def twice(v):
        return np.concatenate([v, v]).reshape(128, 1)

    cols = np.concatenate([
        twice(a["L0_tok_b_k"]), twice(a["L0_attn_bq"]), twice(a["L0_attn_bk"]), twice(a["L0_attn_bo"]),
        a["L0_ffn_b1"].T, a["L0_ffn_b2"].reshape(EPAIRS, 128).T, a["L0_tok_filt"].T, twice(a["L0_attn_bv"])], axis=1)
    qk0 = [a["L0_attn_bq"][0:1]] * 2 + [a["L0_attn_bk"][0:1]] * 2
    rows = np.concatenate([a["L0_ffn_bg"]] * CHUNKS + [a["L0_ffn_bias"]] * CHUNKS + qk0
                          + [np.arange(EXPERTS, dtype=np.float32)] * CHUNKS)
    arrays = {
        "xt": a["x"].reshape(GROUPS, PAIR, LEN, DIN).transpose(0, 3, 1, 2),
        "wtok": a["L0_tok_W_k"].reshape(TAPS, DIN, D).transpose(1, 0, 2),
        "cols": cols,
        "const": constants(),
        "wqk": np.concatenate([a["L0_attn_Wq"].T, a["L0_attn_Wk"].T], axis=1),
        "wv": a["L0_attn_Wv"],
        "wot": a["L0_attn_Wo"].T,
        "rows": np.tile(rows, (128, 1)),
        "bdg": diagonal(a["L0_ffn_Wg"]),
        "w1": a["L0_ffn_W1"].transpose(1, 0, 2),
        "w2": a["L0_ffn_W2"].transpose(1, 0, 2),
    }
    arrays = {k: np.ascontiguousarray(v) for k, v in arrays.items()}
    nc = bacc.Bacc("TRN2", target_bir_lowering=False, num_devices=1)
    aps = [nc.dram_tensor(k, v.shape, F32, kind="ExternalInput").ap() for k, v in arrays.items()]
    out = nc.dram_tensor("out", [GROUPS, 128, WIN], F32, kind="ExternalOutput").ap()
    audio_tower(nc, *aps, out)
    r = run_bass_kernel_spmd(nc, [arrays], core_ids=[0])
    return r.results[0]["out"].reshape(SEQS, D, WIN).transpose(0, 2, 1)
```

```python
from contextlib import ExitStack

import numpy as np
import concourse.bass as bass
from concourse import mybir

F32 = mybir.dt.float32
F32R = mybir.dt.float32r
U32 = mybir.dt.uint32
ALU = mybir.AluOpType
ACT = mybir.ActivationFunctionType
AX = mybir.AxisListType

SEQS, LEN, DIN = 32, 256, 128
TAPS, D = 8, 64
WIN = LEN - TAPS
HALF = WIN // 2
PAIR = 2
GROUPS = SEQS // PAIR
TOK = PAIR * WIN
EXPERTS, HID = 8, 128
EPAIRS = EXPERTS // 2
CHUNKS = 2 * PAIR
VCOLS = PAIR * D + 4
EPS = 1e-5
EXP_LN_SET = 6
KSCALE = D ** -0.5
HTAPS = TAPS // 2
SPAN = WIN + HTAPS

C_BTOK, C_BQ, C_BK, C_BO, C_B1, C_B2, C_FILT, C_BV = 0, 1, 2, 3, 4, 12, 16, 24
NCOLS = 25
R_BG, R_BIAS, R_QK0, R_IOTA = 0, 32, 64, 68
NROWS = 100
K_ID, K_CENTER, K_MEAN, K_FOLD = 0, 128, 256, 384
NCONST = K_FOLD + D


def audio_tower(nc, xt, wtok, cols, const, wqk, wv, wot, rows, bdg, w1, w2, out, weights_dram):
    ctx = ExitStack()
    with ctx:
        def sb(name, shape, dt=F32):
            return ctx.enter_context(nc.sbuf_tensor(name, shape, dt))

        def bank(name):
            return ctx.enter_context(nc.psum_tensor(name, [128, 512], F32))

        def sem(name):
            return ctx.enter_context(nc.semaphore(name))

        wtok_sb = sb("wtok_sb", [128, TAPS, D])
        wconv = sb("wconv", [128, HTAPS, 2, D])
        wconv_hi = sb("wconv_hi", [128, HTAPS, 2 * D], F32R)
        wconv_lo = sb("wconv_lo", [128, HTAPS, 2 * D], F32R)
        col = sb("col", [128, NCOLS])
        row = sb("row", [128, NROWS])
        cst = sb("cst", [128, NCONST])
        bqk = sb("bqk", [128, 1])
        eps = sb("eps", [128, 1])
        warm = sb("warm", [128, 128])
        wqk_sb = sb("wqk_sb", [128, 2 * D])
        wqk_s = sb("wqk_s", [128, 2 * D])
        wqk_hi = sb("wqk_hi", [128, 2 * D], F32R)
        wqk_lo = sb("wqk_lo", [128, 2 * D], F32R)
        wv_sb = sb("wv_sb", [D, D])
        wot_sb = sb("wot_sb", [D, D])
        bv_wide = sb("bv_wide", [D, 128])
        wval = sb("wval", [128, VCOLS])
        bval = sb("bval", [128, VCOLS])
        wg_sb = sb("wg_sb", [128, 2 * EXPERTS])
        w1_sb = sb("w1_sb", [128, EXPERTS, HID])
        w1_hi = sb("w1_hi", [128, EXPERTS, HID], F32R)
        w1_lo = sb("w1_lo", [128, EXPERTS, HID], F32R)
        w2_sb = sb("w2_sb", [HID, EXPERTS, D])
        ident = cst[:, K_ID:K_ID + 128]
        center = cst[:, K_CENTER:K_CENTER + 128]
        meanof = cst[:, K_MEAN:K_MEAN + 128]
        fold = cst[:, K_FOLD:K_FOLD + D]

        x_sb = [sb(f"x{i}", [128, PAIR, LEN]) for i in range(2)]
        x_hi = sb("x_hi", [128, PAIR, LEN], F32R)
        x_lo = sb("x_lo", [128, PAIR, LEN], F32R)
        late = sb("late", [D, PAIR, WIN])
        hsum = sb("hsum", [128, WIN])
        h = [sb(f"h{i}", [128, WIN]) for i in range(2)]
        h2 = [sb(f"h2_{i}", [128, WIN]) for i in range(2)]
        sq = [sb(f"sq{i}", [128, WIN]) for i in range(2)]
        lnv = [sb(f"lnv{i}", [128, WIN]) for i in range(2)]
        rstd = [sb(f"rstd{i}", [128, WIN]) for i in range(2)]
        xn = sb("xn", [128, WIN])
        xn2 = sb("xn2", [128, WIN])
        ts = sb("ts", [128, TOK], F32R)
        xs = [sb(f"xs{i}", [128, TOK], F32R) for i in range(2)]
        qs = sb("qs", [128, TOK], F32R)
        kk = sb("kk", [128, 2, TOK], F32R)
        v_sb = sb("v_sb", [128, 2, VCOLS])
        kmask = sb("kmask", [128, 2, PAIR])
        mask = sb("mask", [128, 2, PAIR])
        nmax = sb("nmax", [128, PAIR, 2])
        psum_p = sb("psum_p", [128, PAIR, 2])
        rsum = sb("rsum", [128, PAIR, 2])
        rmask = sb("rmask", [128, PAIR, 2])
        p_sb = [sb(f"p{b}", [128, 2, WIN]) for b in range(PAIR)]
        pt_sb = [sb(f"pt{b}", [128, 2, WIN]) for b in range(PAIR)]
        lg = sb("lg", [128, CHUNKS, EXPERTS])
        top = sb("top", [128, CHUNKS, 8])
        topi = sb("topi", [128, CHUNKS, 8], U32)
        gbias = sb("gbias", [128, CHUNKS * EXPERTS])
        topf = sb("topf", [128, CHUNKS, 2])
        dlt = sb("dlt", [128, CHUNKS])
        eg = sb("eg", [128, CHUNKS])
        den = sb("den", [128, CHUNKS])
        gw1 = sb("gw1", [128, CHUNKS])
        gw2 = sb("gw2", [128, CHUNKS])
        oh1 = sb("oh1", [128, CHUNKS, EXPERTS])
        oh2 = sb("oh2", [128, CHUNKS, EXPERTS])
        cw1 = sb("cw1", [128, CHUNKS, EXPERTS])
        cw2 = sb("cw2", [128, CHUNKS, EXPERTS])
        cw = sb("cw", [128, EXPERTS, CHUNKS])
        ct_sb = sb("ct_sb", [CHUNKS * EXPERTS, HALF])
        cb = sb("cb", [128, EPAIRS, TOK])
        hid = [sb(f"hid{i}", [128, TOK]) for i in range(4)]
        acc = [sb(f"acc{i}", [128, TOK]) for i in range(2)]
        total = sb("total", [128, TOK])

        bank_h = [bank("bank_h0"), bank("bank_h1")]
        bank_y = [bank("bank_y0"), bank("bank_y1")]
        bank_s = [bank("bank_s0"), bank("bank_s1")]
        bank_a = bank("bank_a")
        bank_b = bank("bank_b")

        par_conv = sem("par_conv")
        par_const = sem("par_const")
        par_attn = sem("par_attn")
        par_moe = sem("par_moe")
        warm_ready = sem("warm_ready")
        set_pool = sem("set_pool")
        set_conv = sem("set_conv")
        set_dve = sem("set_dve")
        set_pe = sem("set_pe")
        passed = sem("passed")
        x_in = [sem("x_in0"), sem("x_in1")]
        o_out = [sem("o_out0"), sem("o_out1")]
        xh_ready = sem("xh_ready")
        xl_ready = sem("xl_ready")
        conv_done = sem("conv_done")
        late_ready = sem("late_ready")
        hsum_ready = sem("hsum_ready")
        h_ready = sem("h_ready")
        cen = [sem("cen1"), sem("cen2")]
        sqr = [sem("sqr1"), sem("sqr2")]
        var = [sem("var1"), sem("var2")]
        lnd = [sem("lnd1"), sem("lnd2")]
        rsd = [sem("rsd1"), sem("rsd2")]
        xn_ready = sem("xn_ready")
        xn2_ready = sem("xn2_ready")
        thi = sem("thi")
        tlo = sem("tlo")
        xhi = sem("xhi")
        xlo = sem("xlo")
        qk_done = sem("qk_done")
        qkh_ready = sem("qkh_ready")
        qkl_ready = sem("qkl_ready")
        k_copied = sem("k_copied")
        v_done = sem("v_done")
        v_ready = sem("v_ready")
        kmask_ready = sem("kmask_ready")
        mask_ready = sem("mask_ready")
        sc_done = sem("sc_done")
        nmax_ready = sem("nmax_ready")
        ex_ready = sem("ex_ready")
        rs_ready = sem("rs_ready")
        rm_ready = sem("rm_ready")
        p_ready = sem("p_ready")
        pt_done = sem("pt_done")
        pt_ready = sem("pt_ready")
        pv_done = sem("pv_done")
        h2_ready = sem("h2_ready")
        gate_done = sem("gate_done")
        topk = sem("topk")
        dlt_ready = sem("dlt_ready")
        eg_ready = sem("eg_ready")
        ct_done = sem("ct_done")
        ct_ready = sem("ct_ready")
        cb_in = [sem("cb_in0"), sem("cb_in1")]
        ct_stored = sem("ct_stored")
        l1_done = sem("l1_done")
        hid_ready = [sem("hid_even"), sem("hid_odd")]
        y_done = sem("y_done")
        acc_ready = sem("acc_ready")
        sum_ready = sem("sum_ready")
        fin_done = sem("fin_done")
        out_ready = sem("out_ready")

        WARMUP = 12
        N_CONV, N_ATTN, N_MOE = 2, 5, 4
        TOPK = 10

        def after(eng, s, value):
            if not isinstance(value, int) or value > 0:
                eng.wait_ge(s, value)

        def hold(eng, s, value):
            eng.wait_ge(s, value)
            eng.sem_inc(passed, 1)

        def after_hold(eng, s, value):
            if not isinstance(value, int) or value > 0:
                hold(eng, s, value)

        def run(iteration, eng):
            iteration(-2, 0, True, False, False, False, False)
            iteration(-1, 1, True, True, False, False, False)
            iteration(0, 0, True, True, True, False, False)
            iteration(1, 1, True, True, True, True, False)
            with eng.Fori(0, (GROUPS - 4) // 2) as i:
                iteration(i * 2 + 2, 0, True, True, True, True, True)
                iteration(i * 2 + 3, 1, True, True, True, True, True)
            iteration(GROUPS - 2, 0, False, True, True, True, True)
            iteration(GROUPS - 1, 1, False, False, True, True, True)
            iteration(GROUPS, 0, False, False, False, True, True)
            iteration(GROUPS + 1, 1, False, False, False, False, True)

        def low_parts(eng, dst, src):
            eng.tensor_tensor(dst[D:128, 0:WIN], src[0:D, :], dst[0:D, 0:WIN].bitcast(F32), ALU.subtract)
            return eng.tensor_tensor(dst[0:D, WIN:TOK], src[D:128, :], dst[D:128, WIN:TOK].bitcast(F32),
                                     ALU.subtract)

        def add(eng, m, p):
            eng.wait_ge(acc_ready, 4 * m + p + 1)
            if p == 1:
                after(eng, fin_done, m)
                eng.tensor_tensor(total[:, :], acc[0][:, :], acc[1][:, :], ALU.add).then_inc(sum_ready, 1)
            else:
                eng.wait_ge(sum_ready, 3 * m + p - 1)
                eng.tensor_tensor(total[:, :], total[:, :], acc[p % 2][:, :], ALU.add).then_inc(sum_ready, 1)

        block = ctx.enter_context(nc.Block())

        @block.sync
        def _(sp):
            sp.dma_start(wtok_sb[:, :, :], wtok).then_inc(par_conv, 16)
            sp.dma_start(cst[:, :], const).then_inc(par_const, 16)
            for dst, src in ((wqk_sb[0:D, :], wqk), (wqk_sb[D:128, :], wqk), (wv_sb[:, :], wv), (wot_sb[:, :], wot),
                             (row[:, :], rows)):
                sp.dma_start(dst, src).then_inc(par_attn, 16)
            for dst, src in ((w1_sb[0:D, :, :], w1), (w1_sb[D:128, :, :], w1), (w2_sb[:, :, :], w2),
                             (wg_sb[:, :], bdg)):
                sp.dma_start(dst, src).then_inc(par_moe, 16)

            def store_weights(m):
                hold(sp, ct_ready, m + 1)
                for half in range(2):
                    after_hold(sp, cb_in[half], 32 * m)
                sp.dma_start(weights_dram.rearrange("e (j t) -> (e j) t", j=CHUNKS),
                             ct_sb[:, :]).then_inc(ct_stored, 16)

            def spread(m, half):
                if half == 0:
                    hold(sp, ct_stored, 16 * m + 16)
                    after_hold(sp, acc_ready, 4 * m)
                for s in range(2):
                    src = weights_dram.rearrange("(p s) t -> s p t", s=2)[s:s + 1, 2 * half:2 * half + 2, :]
                    sp.dma_start(cb[s * D:s * D + D, 2 * half:2 * half + 2, :],
                                 src.to_broadcast([D, 2, TOK])).then_inc(cb_in[half], 16)

            def iteration(t, odd, d_, c_, n_, m_, f_):
                d, c, m, f = t + 2, t + 1, t - 1, t - 2
                if d_:
                    after_hold(sp, xh_ready, d - 1)
                    after_hold(sp, xl_ready, d - 1)
                    if not (isinstance(t, int) and d == 0):
                        sp.dma_start(x_sb[odd][:, :, :], xt[d]).then_inc(x_in[odd], 16)
                if m_:
                    store_weights(m)
                if f_:
                    hold(sp, out_ready, f + 1)
                    sp.dma_start(out[f], h2[odd][:, :]).then_inc(o_out[odd], 16)
                if m_:
                    spread(m, 0)
                    spread(m, 1)
                if c_:
                    hold(sp, qkl_ready, 2 * c + 2)
                    sp.dma_start(kk[0:D, :, :].bitcast(F32), kk[D:128, :, :].bitcast(F32)).then_inc(k_copied, 16)

            run(iteration, sp)
            for i in range(2):
                sp.wait_ge(o_out[i], 16 * GROUPS // 2)

        @block.gpsimd
        def _(pool):
            pool.memset(eps[:, :], EPS).then_inc(set_pool, 1)

            def scale(n, b):
                pool.wait_ge(rm_ready, 2 * n + b + 1)
                pool.tensor_tensor(p_sb[b][0:HALF, :, :], p_sb[b][0:HALF, :, :],
                                   rmask[0:HALF, b, :].unsqueeze(2).to_broadcast([HALF, 2, WIN]),
                                   ALU.mult).then_inc(p_ready, 1)

            def iteration(t, odd, d_, c_, n_, m_, f_):
                d, n, m, f = t + 2, t, t - 1, t - 2
                if f_:
                    add(pool, f, 2)
                if n_:
                    scale(n, 0)
                    scale(n, 1)
                if d_:
                    pool.wait_ge(xh_ready, d + 1)
                    pool.tensor_tensor(x_lo[:, :, :], x_sb[odd][:, :, :], x_hi[:, :, :].bitcast(F32),
                                       ALU.subtract).then_inc(xl_ready, 1)
                if m_:
                    add(pool, m, 1)

            run(iteration, pool)

        @block.scalar
        def _(act):
            act.add_instruction(mybir.InstLoadActFuncSet(
                name=nc.get_next_instruction_name(), engine=mybir.EngineType.Activation, ins=[], outs=[],
                act_func_set_id=EXP_LN_SET))
            act.dma_start(col[:, :], cols).then_inc(par_conv, 16)
            act.dma_start(x_sb[0][:, :, :], xt[0]).then_inc(x_in[0], 16)

            def exps(n, b):
                act.wait_ge(nmax_ready, 2 * n + b + 1)
                after(act, pt_done, 2 * n + b - 1)
                after(act, rs_ready, 2 * n + b - 1)
                for i in range(2):
                    last = act.activation(p_sb[b][0:HALF, i, :], bank_s[b][0:HALF, i * WIN:(i + 1) * WIN], ACT.Exp,
                                          bias=nmax[0:HALF, b, i:i + 1], accum_out=psum_p[0:HALF, b, i:i + 1])
                last.then_inc(ex_ready, 1)

            def relu(m, e):
                p, s = e // 2, e % 2
                act.wait_ge(l1_done, 8 * m + e + 1)
                after(act, y_done, 4 * m + p - 1)
                act.activation(hid[2 * (p % 2) + s][:, :], bank_h[s][:, 0:TOK], ACT.Relu,
                               bias=col[:, C_B1 + e:C_B1 + e + 1]).then_inc(hid_ready[s], 1)

            def square(g, which, src):
                act.wait_ge(cen[which], g + 1)
                after(act, var[which], g)
                act.activation(sq[which][:, :], src[:, 0:WIN], ACT.Square).then_inc(sqr[which], 1)

            def rsqrt(g, which, src, used):
                act.wait_ge(var[which], g + 1)
                act.activation(lnv[which][:, :], src[:, WIN:2 * WIN], ACT.Ln, bias=eps[:, :]).then_inc(lnd[which], 1)
                act.wait_ge(lnd[which], g + 1)
                after(act, used, g)
                act.activation(rstd[which][:, :], lnv[which][:, :], ACT.Exp, scale=-0.5).then_inc(rsd[which], 1)

            def high_parts(dst, src):
                act.activation(dst[0:D, 0:WIN], src[0:D, :], ACT.Copy)
                return act.activation(dst[D:128, WIN:TOK], src[D:128, :], ACT.Copy)

            def turned(n, b):
                act.wait_ge(pt_done, 2 * n + b + 1)
                after(act, pv_done, n)
                act.activation(pt_sb[b][0:HALF, :, :], bank_s[b][0:HALF, 0:TOK].rearrange("p (a b) -> p a b", a=2),
                               ACT.Copy).then_inc(pt_ready, 1)

            def later_taps(c):
                act.wait_ge(conv_done, c + 1)
                after(act, hsum_ready, c)
                act.activation(late[:, :, :],
                               bank_a[D:128, 0:PAIR * SPAN].rearrange("p (a b) -> p a b", a=PAIR)[:, :, HTAPS:SPAN],
                               ACT.Identity, bias=col[D:128, C_BTOK:C_BTOK + 1]).then_inc(late_ready, 1)

            def high_queries_keys(c):
                act.wait_ge(qk_done, c + 1)
                after(act, sc_done, 2 * c)
                act.activation(qs[0:D, :], bank_b[0:D, 0:TOK], ACT.Identity, bias=bqk[0:D, :])
                act.activation(kk[D:128, 0, :], bank_b[D:128, 0:TOK], ACT.Identity,
                               bias=bqk[D:128, :]).then_inc(qkh_ready, 1)

            act.wait_ge(par_conv, 16 * N_CONV)
            act.wait_ge(set_pool, 1)

            def iteration(t, odd, d_, c_, n_, m_, f_):
                d, c, n, m = t + 2, t + 1, t, t - 1
                if m_:
                    relu(m, 1)
                if n_:
                    exps(n, 1)
                if m_:
                    relu(m, 2)
                    relu(m, 3)
                if c_:
                    rsqrt(c, 0, bank_b, xn_ready)
                if d_:
                    act.wait_ge(x_in[odd], 8 * (d - odd) + 16)
                    after(act, conv_done, d)
                    act.activation(x_hi[:, :, :], x_sb[odd][:, :, :], ACT.Copy).then_inc(xh_ready, 1)
                if c_:
                    act.wait_ge(xn_ready, c + 1)
                    after(act, qk_done, c)
                    high_parts(ts, xn).then_inc(thi, 1)
                if n_:
                    turned(n, 0)
                    turned(n, 1)
                if m_:
                    relu(m, 4)
                if c_:
                    high_queries_keys(c)
                if n_:
                    square(n, 1, bank_s[0])
                if m_:
                    relu(m, 5)
                if n_:
                    rsqrt(n, 1, bank_s[0], xn2_ready)
                if d_:
                    later_taps(d)
                if n_:
                    act.wait_ge(xn2_ready, n + 1)
                    after(act, l1_done, 8 * (n - 1))
                    high_parts(xs[odd], xn2).then_inc(xhi, 1)
                if m_:
                    relu(m, 6)
                if d_:
                    act.wait_ge(hsum_ready, d + 1)
                    after(act, h2_ready, d - 1)
                    act.activation(h[odd][:, :], hsum[:, :], ACT.Relu).then_inc(h_ready, 1)
                if m_:
                    relu(m, 7)
                if n_:
                    act.wait_ge(dlt_ready, n + 1)
                    act.activation(eg[0:HALF, :], dlt[0:HALF, :], ACT.Exp).then_inc(eg_ready, 1)
                    relu(n, 0)
                if d_:
                    square(d, 0, bank_b)
                if c_:
                    exps(c, 0)

            run(iteration, act)

        @block.vector
        def _(dve):
            dve.memset(warm[:, :], 0.0).then_inc(warm_ready, 1)
            dve.wait_ge(par_conv, 16 * N_CONV)
            dve.tensor_tensor(wconv[:, :, :, :], wtok_sb[:, :, :].rearrange("p (s f) k -> p f s k", s=2),
                              col[:, C_FILT:C_FILT + TAPS].rearrange("p (s f) -> p f s", s=2).unsqueeze(3)
                              .to_broadcast([128, HTAPS, 2, D]), ALU.mult).then_inc(set_conv, 1)
            dve.wait_ge(set_conv, 1)
            wide_w = wconv[:, :, :, :].rearrange("p f s k -> p f (s k)")
            dve.tensor_copy(wconv_hi[:, :, :], wide_w).then_inc(set_conv, 1)
            dve.wait_ge(set_conv, 2)
            dve.tensor_tensor(wconv_lo[:, :, :], wide_w, wconv_hi[:, :, :].bitcast(F32),
                              ALU.subtract).then_inc(set_conv, 1)

            def attention_parameters():
                dve.wait_ge(par_attn, 16 * N_ATTN)
                dve.tensor_copy(bqk[0:D, :], col[0:D, C_BQ:C_BQ + 1])
                dve.tensor_scalar(bqk[D:128, :], col[D:128, C_BK:C_BK + 1], KSCALE, None, ALU.mult)
                dve.tensor_copy(bv_wide[:, :], col[0:D, C_BV:C_BV + 1].to_broadcast([D, 128]))
                dve.tensor_copy(wqk_s[:, 0:D], wqk_sb[:, 0:D])
                dve.tensor_scalar(wqk_s[:, D:], wqk_sb[:, D:], KSCALE, None, ALU.mult).then_inc(set_dve, 1)
                dve.wait_ge(set_dve, 1)
                dve.tensor_copy(wqk_hi[:, :], wqk_s[:, :])
                dve.memset(wval[:, :], 0.0).then_inc(set_dve, 1)
                dve.wait_ge(set_dve, 2)
                dve.tensor_tensor(wqk_lo[:, :], wqk_s[:, :], wqk_hi[:, :].bitcast(F32), ALU.subtract)
                for j in range(2):
                    rows_j = slice(j * D, j * D + D)
                    dve.tensor_copy(wval[rows_j, 128 + j:129 + j], wqk_sb[rows_j, 0:1])
                    dve.tensor_copy(wval[rows_j, 130 + j:131 + j], wqk_sb[rows_j, D:D + 1])
                dve.tensor_tensor(gbias[:, :], row[:, R_BG:R_BG + 32], row[:, R_BIAS:R_BIAS + 32], ALU.add)
                dve.tensor_copy(bval[:, PAIR * D:VCOLS], row[:, R_QK0:R_QK0 + 4]).then_inc(set_dve, 1)

            def value_weights():
                dve.wait_ge(set_pe, 1)
                for b in range(PAIR):
                    rows_b = slice(b * D, b * D + D)
                    dve.tensor_copy(wval[rows_b, b * D:b * D + D], bank_y[0][rows_b, 0:D])
                    last = dve.tensor_copy(bval[:, b * D:b * D + D], bank_y[0][:, D:2 * D])
                last.then_inc(set_dve, 1)

            def expert_parameters():
                dve.wait_ge(par_moe, 16 * N_MOE)
                dve.tensor_copy(w1_hi[:, :, :], w1_sb[:, :, :]).then_inc(set_dve, 1)
                dve.wait_ge(set_dve, 5)
                dve.tensor_tensor(w1_lo[:, :, :], w1_sb[:, :, :], w1_hi[:, :, :].bitcast(F32),
                                  ALU.subtract).then_inc(set_dve, 1)

            def relu(m, e):
                p, s = e // 2, e % 2
                dve.wait_ge(l1_done, 8 * m + e + 1)
                after(dve, y_done, 4 * m + p - 1)
                dve.tensor_scalar(hid[2 * (p % 2) + s][:, :], bank_h[s][:, 0:TOK],
                                  col[:, C_B1 + e:C_B1 + e + 1], 0.0, ALU.add, ALU.max).then_inc(hid_ready[s], 1)

            def weigh(m, p):
                dve.wait_ge(y_done, 4 * m + p + 1)
                dve.wait_ge(cb_in[p // 2], 32 * m + 32)
                after(dve, sum_ready, 3 * m + (-1, 0, 1, 1)[p])
                dve.scalar_tensor_tensor(out=acc[p % 2][:, :], in0=bank_y[p % 2][:, 0:TOK],
                                         scalar=col[:, C_B2 + p:C_B2 + p + 1], in1=cb[:, p, :], op0=ALU.add,
                                         op1=ALU.mult).then_inc(acc_ready, 1)

            def rowmax(n, b):
                dve.wait_ge(sc_done, 2 * n + b + 1)
                after(dve, ex_ready, 2 * n + b - 1)
                dve.tensor_reduce(nmax[0:HALF, b, :], bank_s[b][0:HALF, 0:TOK].rearrange("p (a b) -> p a b", a=2),
                                  AX.X, ALU.max, negate=True).then_inc(nmax_ready, 1)

            def recip(n, b):
                dve.wait_ge(ex_ready, 2 * n + b + 1)
                after(dve, p_ready, 2 * n + b - 1)
                dve.reciprocal(rsum[0:HALF, b, :], psum_p[0:HALF, b, :]).then_inc(rs_ready, 1)
                dve.wait_ge(rs_ready, 2 * n + b + 1)
                dve.wait_ge(mask_ready, n + 1)
                dve.tensor_tensor(rmask[0:HALF, b, :], rsum[0:HALF, b, :], mask[0:HALF, :, b],
                                  ALU.mult).then_inc(rm_ready, 1)

            T = slice(0, HALF)

            def by_chunk(a):
                return a.rearrange("p (a b) -> p a b", a=CHUNKS)

            def wide(a):
                return a.unsqueeze(2).to_broadcast([HALF, CHUNKS, EXPERTS])

            def seen(m, k):
                dve.wait_ge(topk, TOPK * m + k)

            def logits(m):
                dve.wait_ge(gate_done, m + 1)
                dve.tensor_tensor(lg[T, :, :].rearrange("p (b i) e -> p i b e", b=PAIR),
                                  bank_s[0][T, 0:CHUNKS * EXPERTS].rearrange("p (i b e) -> p i b e", i=2, b=PAIR),
                                  gbias[T, :].rearrange("p (i b e) -> p i b e", i=2, b=PAIR), ALU.add).then_inc(topk, 1)

            def largest(m):
                hold(dve, topk, TOPK * m + 1)
                for j in range(CHUNKS):
                    last = dve.max(top[T, j, :], lg[T, j, :])
                last.then_inc(topk, 1)

            def difference(m):
                seen(m, 2)
                dve.tensor_tensor(dlt[T, :], top[T, :, 1], top[T, :, 0], ALU.subtract).then_inc(dlt_ready, 1)

            def indices(m):
                for j in range(CHUNKS):
                    last = dve.max_index(topi[T, j, :], top[T, j, :], lg[T, j, :])
                last.then_inc(topk, 1)

            def denominator(m):
                seen(m, 3)
                dve.tensor_copy(topf[T, :, :], topi[T, :, 0:2]).then_inc(topk, 1)
                dve.wait_ge(eg_ready, m + 1)
                dve.tensor_scalar(den[T, :], eg[T, :], 1.0, None, ALU.add).then_inc(topk, 1)

            def one_hot(m):
                iota = by_chunk(row[T, R_IOTA:R_IOTA + 32])
                seen(m, 5)
                dve.reciprocal(gw1[T, :], den[T, :]).then_inc(topk, 1)
                dve.tensor_tensor(oh1[T, :, :], iota, wide(topf[T, :, 0]), ALU.is_equal)
                dve.tensor_tensor(oh2[T, :, :], iota, wide(topf[T, :, 1]), ALU.is_equal).then_inc(topk, 1)

            def weights(m):
                seen(m, 6)
                dve.tensor_tensor(gw2[T, :], eg[T, :], gw1[T, :], ALU.mult).then_inc(topk, 1)
                seen(m, 7)
                dve.tensor_tensor(cw1[T, :, :], oh1[T, :, :], wide(gw1[T, :]), ALU.mult)

            def second_weight(m):
                seen(m, 8)
                dve.tensor_tensor(cw2[T, :, :], oh2[T, :, :], wide(gw2[T, :]), ALU.mult).then_inc(topk, 1)

            def both_weights(m):
                seen(m, 9)
                after(dve, ct_done, m)
                dve.tensor_tensor(cw[T, :, :].rearrange("p e j -> p j e"), cw1[T, :, :], cw2[T, :, :],
                                  ALU.add).then_inc(topk, 1)

            def both_taps(c):
                dve.wait_ge(late_ready, c + 1)
                after(dve, h_ready, c)
                for b in range(PAIR):
                    last = dve.tensor_tensor(hsum[b * D:b * D + D, :], bank_a[0:D, b * SPAN:b * SPAN + WIN],
                                             late[:, b, :], ALU.add)
                last.then_inc(hsum_ready, 1)

            def keep_weights(m):
                dve.wait_ge(ct_done, m + 1)
                after(dve, ct_stored, 16 * m)
                dve.tensor_copy(ct_sb[:, :], bank_a[0:CHUNKS * EXPERTS, WIN:WIN + HALF]).then_inc(ct_ready, 1)

            def normalise(c):
                dve.wait_ge(rsd[0], c + 1)
                after(dve, v_done, c)
                after(dve, tlo, c)
                dve.tensor_tensor(xn[:, :], bank_b[:, 0:WIN], rstd[0][:, :], ALU.mult).then_inc(xn_ready, 1)

            def normalise_2(n):
                dve.wait_ge(rsd[1], n + 1)
                after(dve, gate_done, n)
                after(dve, xlo, n)
                dve.tensor_tensor(xn2[:, :], bank_s[0][:, 0:WIN], rstd[1][:, :], ALU.mult).then_inc(xn2_ready, 1)

            def keep_values(c):
                dve.wait_ge(v_done, c + 1)
                after(dve, pv_done, c)
                dve.tensor_tensor(v_sb[0:HALF, :, :],
                                  bank_s[1][0:HALF, 0:2 * VCOLS].rearrange("p (a b) -> p a b", a=2),
                                  bval[0:HALF, :].unsqueeze(1).to_broadcast([HALF, 2, VCOLS]),
                                  ALU.add).then_inc(v_ready, 1)

            def low_queries(c):
                dve.wait_ge(qkh_ready, c + 1)
                dve.scalar_tensor_tensor(out=qs[D:128, :], in0=bank_b[0:D, 0:TOK], scalar=bqk[0:D, :],
                                         in1=qs[0:D, :].bitcast(F32), op0=ALU.add,
                                         op1=ALU.subtract).then_inc(qkl_ready, 1)

            def low_keys(c):
                dve.wait_ge(qkh_ready, c + 1)
                dve.scalar_tensor_tensor(out=kk[D:128, 1, :], in0=bank_b[D:128, 0:TOK], scalar=bqk[D:128, :],
                                         in1=kk[D:128, 0, :].bitcast(F32), op0=ALU.add,
                                         op1=ALU.subtract).then_inc(qkl_ready, 1)

            def masks(c):
                dve.wait_ge(v_ready, c + 1)
                dve.tensor_scalar(kmask[0:HALF, :, :], v_sb[0:HALF, :, 130:132], 0.0, None,
                                  ALU.not_equal).then_inc(kmask_ready, 1)
                dve.wait_ge(kmask_ready, c + 1)
                dve.scalar_tensor_tensor(out=mask[0:HALF, :, :], in0=v_sb[0:HALF, :, 128:130], scalar=0.0,
                                         in1=kmask[0:HALF, :, :], op0=ALU.not_equal,
                                         op1=ALU.mult).then_inc(mask_ready, 1)

            def iteration(t, odd, d_, c_, n_, m_, f_):
                d, c, n, m, f = t + 2, t + 1, t, t - 1, t - 2
                if f_:
                    weigh(f, 3)
                if m_:
                    keep_weights(m)
                if f_:
                    add(dve, f, 3)
                if n_:
                    recip(n, 1)
                if c_:
                    normalise(c)
                if f_:
                    dve.wait_ge(fin_done, f + 1)
                    dve.tensor_tensor(h2[odd][:, :], bank_a[:, 0:WIN], h2[odd][:, :], ALU.add).then_inc(out_ready, 1)
                if c_:
                    dve.wait_ge(thi, c + 1)
                    low_parts(dve, ts, xn).then_inc(tlo, 1)
                    if isinstance(t, int) and c == 0:
                        value_weights()
                if n_:
                    dve.wait_ge(pv_done, n + 1)
                    after(dve, o_out[odd], 8 * (n - odd))
                    dve.scalar_tensor_tensor(out=h2[odd][:, :], in0=bank_s[0][:, 0:WIN], scalar=col[:, C_BO:C_BO + 1],
                                             in1=h[odd][:, :], op0=ALU.add, op1=ALU.add).then_inc(h2_ready, 1)
                if c_:
                    low_queries(c)
                    low_keys(c)
                    if isinstance(t, int) and c == 0:
                        expert_parameters()
                if m_:
                    weigh(m, 0)
                    weigh(m, 1)
                if c_:
                    keep_values(c)
                if n_:
                    normalise_2(n)
                if c_:
                    masks(c)
                if d_:
                    both_taps(d)
                    if isinstance(t, int) and d == 0:
                        attention_parameters()
                if n_:
                    logits(n)
                    dve.wait_ge(xhi, n + 1)
                    low_parts(dve, xs[odd], xn2).then_inc(xlo, 1)
                    largest(n)
                    difference(n)
                    indices(n)
                if c_:
                    rowmax(c, 0)
                if n_:
                    denominator(n)
                if m_:
                    weigh(m, 2)
                if n_:
                    one_hot(n)
                if c_:
                    rowmax(c, 1)
                if n_:
                    weights(n)
                    second_weight(n)
                if c_:
                    recip(c, 0)
                if n_:
                    both_weights(n)

            run(iteration, dve)

        @block.tensor
        def _(pe):
            def bounded(groups):
                return min(groups, GROUPS) if isinstance(groups, int) else groups

            def conv(c, steps):
                passes = [(w, x, j) for w, x in ((wconv_hi, x_hi), (wconv_lo, x_hi), (wconv_hi, x_lo))
                          for j in range(HTAPS)]
                for k in steps:
                    w, x, j = passes[k]
                    if k == 0:
                        pe.wait_ge(xh_ready, c + 1)
                        after(pe, hsum_ready, c)
                        after(pe, ct_ready, c - 2)
                        after(pe, out_ready, c - 3)
                    if isinstance(c, int) and c == 0 and k == HTAPS:
                        pe.wait_ge(set_conv, 3)
                    if k == 2 * HTAPS:
                        pe.wait_ge(xl_ready, c + 1)
                    last = pe.matmul(bank_a[:, 0:PAIR * SPAN].rearrange("p (a b) -> p a b", a=PAIR), w[:, j, :],
                                     x[:, :, j:j + SPAN], start=(k == 0), stop=(k == len(passes) - 1))
                if len(passes) - 1 in steps:
                    last.then_inc(conv_done, 1)

            def scores(n, b):
                pe.wait_ge(k_copied, 16 * n + 16)
                pe.wait_ge(qkl_ready, 2 * n + 2)
                if b == 0:
                    after(pe, topk, TOPK * (n - 1) + 1)
                else:
                    pe.wait_ge(v_ready, n + 1)
                for i in range(2):
                    for part in range(2):
                        last = pe.matmul(bank_s[b][0:HALF, i * WIN:(i + 1) * WIN],
                                         qs[:, b * WIN + i * HALF:b * WIN + (i + 1) * HALF],
                                         kk[:, part, b * WIN:(b + 1) * WIN], start=(part == 0), stop=(part == 1))
                last.then_inc(sc_done, 1)

            def turn_p(n, b):
                pe.wait_ge(p_ready, 2 * n + b + 1)
                for j in range(2):
                    for i in range(2):
                        at = j * WIN + i * HALF
                        last = pe.transpose(bank_s[b][0:HALF, at:at + HALF],
                                            p_sb[b][0:HALF, i, j * HALF:(j + 1) * HALF], ident[0:HALF, 0:HALF])
                last.then_inc(pt_done, 1)

            def turn_weights(m):
                pe.wait_ge(topk, TOPK * m + TOPK)
                pe.wait_ge(hsum_ready, bounded(m + 3))
                if isinstance(m, int) and m + 2 >= GROUPS:
                    pe.wait_ge(ct_ready, m)
                pe.transpose(bank_a[0:CHUNKS * EXPERTS, WIN:WIN + HALF], cw[0:HALF, :, :].rearrange("p e j -> p (e j)"),
                             ident[0:HALF, 0:HALF]).then_inc(ct_done, 1)

            def hidden(m, par, e):
                if e == 0:
                    pe.wait_ge(xhi, m + 1)
                    pe.wait_ge(xlo, m + 1)
                after(pe, hid_ready[e % 2], 4 * m + e // 2)
                pe.matmul(bank_h[e % 2][:, 0:TOK], w1_hi[:, e, :], xs[par][:, :], start=True, stop=False)
                pe.matmul(bank_h[e % 2][:, 0:TOK], w1_lo[:, e, :], xs[par][:, :], start=False,
                          stop=True).then_inc(l1_done, 1)

            def expert_out(m, p):
                pe.wait_ge(hid_ready[0], 4 * m + p + 1)
                pe.wait_ge(hid_ready[1], 4 * m + p + 1)
                after(pe, acc_ready, 4 * m + p - 1)
                for s in range(2):
                    last = pe.matmul(bank_y[p % 2][s * D:s * D + D, 0:TOK], w2_sb[:, 2 * p + s, :],
                                     hid[2 * (p % 2) + s][:, :], start=True, stop=True)
                last.then_inc(y_done, 1)

            def centre(g, which, dst, src):
                pe.matmul(dst[:, 0:WIN], center, src[:, :], start=True, stop=True).then_inc(cen[which], 1)

            def variance(g, which, dst):
                pe.wait_ge(sqr[which], g + 1)
                pe.matmul(dst[:, WIN:2 * WIN], meanof, sq[which][:, :], start=True, stop=True).then_inc(var[which], 1)

            def parameter_products():
                pe.wait_ge(par_attn, 16 * N_ATTN)
                pe.wait_ge(set_dve, 3)
                for b in range(PAIR):
                    pe.matmul(bank_y[0][b * D:b * D + D, 0:D], wv_sb[:, :], wot_sb[:, :], start=True, stop=True)
                pe.matmul(bank_y[0][:, D:2 * D], bv_wide[:, :], wot_sb[:, :], start=True, stop=True).then_inc(set_pe, 1)

            pe.wait_ge(warm_ready, 1)
            for _ in range(WARMUP):
                pe.matmul(bank_h[0][:, 0:128], warm[:, :], warm[:, :], start=True, stop=True)
            pe.wait_ge(set_conv, 2)

            def fold_halves(f):
                pe.wait_ge(sum_ready, 3 * f + 3)
                pe.wait_ge(hsum_ready, bounded(f + 4))
                pe.wait_ge(ct_ready, bounded(f + 2))
                if isinstance(f, int) and f + 3 >= GROUPS:
                    pe.wait_ge(out_ready, f)
                for b in range(PAIR):
                    last = pe.matmul(bank_a[b * D:b * D + D, 0:WIN], fold, total[:, b * WIN:(b + 1) * WIN],
                                     start=True, stop=True)
                last.then_inc(fin_done, 1)

            def first_centre(c, par):
                if isinstance(c, int) and c == 0:
                    pe.wait_ge(par_const, 16)
                pe.wait_ge(h_ready, c + 1)
                after(pe, qkl_ready, 2 * c)
                centre(c, 0, bank_b, h[par])

            def attend(n):
                pe.wait_ge(pt_ready, 2 * n + 2)
                for j in range(2):
                    for b in range(PAIR):
                        last = pe.matmul(bank_s[0][b * D:b * D + D, 0:WIN], v_sb[0:HALF, j, b * D:b * D + D],
                                         pt_sb[b][0:HALF, j, :], start=(j == 0), stop=(j == 1))
                last.then_inc(pv_done, 1)

            def queries_keys(c):
                pe.wait_ge(thi, c + 1)
                pe.wait_ge(tlo, c + 1)
                pe.matmul(bank_b[:, 0:TOK], wqk_hi[:, :], ts[:, :], start=True, stop=False)
                pe.matmul(bank_b[:, 0:TOK], wqk_lo[:, :], ts[:, :], start=False, stop=True).then_inc(qk_done, 1)

            def values(c):
                if isinstance(c, int) and c == 0:
                    pe.wait_ge(set_dve, 4)
                pe.wait_ge(xn_ready, c + 1)
                after(pe, pt_ready, 2 * c)
                for i in range(2):
                    last = pe.matmul(bank_s[1][0:HALF, i * VCOLS:(i + 1) * VCOLS], xn[:, i * HALF:(i + 1) * HALF],
                                     wval[:, :], start=True, stop=True)
                last.then_inc(v_done, 1)

            def iteration(t, odd, d_, c_, n_, m_, f_):
                d, c, n, m, f = t + 2, t + 1, t, t - 1, t - 2
                even = 1 - odd
                if c_:
                    first_centre(c, even)
                if n_:
                    scores(n, 1)
                if m_:
                    hidden(m, even, 1)
                if f_:
                    expert_out(f, 3)
                if c_:
                    variance(c, 0, bank_b)
                if m_:
                    hidden(m, even, 2)
                    hidden(m, even, 3)
                    turn_weights(m)
                    expert_out(m, 0)
                if n_:
                    turn_p(n, 0)
                if f_:
                    fold_halves(f)
                if m_:
                    expert_out(m, 1)
                if n_:
                    turn_p(n, 1)
                if m_:
                    hidden(m, even, 4)
                if d_:
                    conv(d, range(0, 2))
                if c_:
                    if isinstance(t, int) and c == 0:
                        parameter_products()
                    queries_keys(c)
                if n_:
                    attend(n)
                if d_:
                    conv(d, range(2, 4))
                if m_:
                    hidden(m, even, 5)
                if d_:
                    conv(d, range(4, 6))
                if n_:
                    pe.wait_ge(h2_ready, n + 1)
                    centre(n, 1, bank_s[0], h2[odd])
                if d_:
                    conv(d, range(6, 10))
                if n_:
                    variance(n, 1, bank_s[0])
                if c_:
                    values(c)
                if d_:
                    conv(d, range(10, 12))
                if m_:
                    hidden(m, even, 6)
                    hidden(m, even, 7)
                if n_:
                    pe.wait_ge(xn2_ready, n + 1)
                    if isinstance(t, int) and n == 0:
                        pe.wait_ge(par_moe, 16 * N_MOE)
                        pe.wait_ge(set_dve, 6)
                    for i in range(2):
                        last = pe.matmul(bank_s[0][0:HALF, i * 16:i * 16 + 16], xn2[:, i * HALF:(i + 1) * HALF],
                                         wg_sb[:, :], start=True, stop=True)
                    last.then_inc(gate_done, 1)
                if m_:
                    expert_out(m, 2)
                if c_:
                    scores(c, 0)
                if n_:
                    hidden(n, odd, 0)

            run(iteration, pe)


def constants():
    half = np.arange(128) // D
    same = (half[:, None] == half[None, :]).astype(np.float32)
    eye = np.eye(128, dtype=np.float32)
    return np.concatenate([eye, eye - same / D, same / D, np.tile(np.eye(D, dtype=np.float32), (2, 1))],
                          axis=1).astype(np.float32)


NAMES = ("x", "L0_tok_filt", "L0_tok_W_k", "L0_tok_b_k", "L0_attn_Wq", "L0_attn_bq", "L0_attn_Wk", "L0_attn_bk",
         "L0_attn_Wv", "L0_attn_bv", "L0_attn_Wo", "L0_attn_bo", "L0_ffn_Wg", "L0_ffn_bg", "L0_ffn_bias",
         "L0_ffn_W1", "L0_ffn_b1", "L0_ffn_W2", "L0_ffn_b2")


def kernel(x, L0_tok_filt, L0_tok_W_k, L0_tok_b_k, L0_attn_Wq, L0_attn_bq, L0_attn_Wk, L0_attn_bk, L0_attn_Wv,
           L0_attn_bv, L0_attn_Wo, L0_attn_bo, L0_ffn_Wg, L0_ffn_bg, L0_ffn_bias, L0_ffn_W1, L0_ffn_b1, L0_ffn_W2,
           L0_ffn_b2):
    import concourse.bacc as bacc
    from concourse.bass_utils import run_bass_kernel_spmd

    a = {k: np.asarray(v) for k, v in zip(NAMES, (
        x, L0_tok_filt, L0_tok_W_k, L0_tok_b_k, L0_attn_Wq, L0_attn_bq, L0_attn_Wk, L0_attn_bk, L0_attn_Wv,
        L0_attn_bv, L0_attn_Wo, L0_attn_bo, L0_ffn_Wg, L0_ffn_bg, L0_ffn_bias, L0_ffn_W1, L0_ffn_b1, L0_ffn_W2,
        L0_ffn_b2))}

    def diagonal(w):
        out = np.zeros((2 * D, 2 * w.shape[1]), w.dtype)
        out[0:D, 0:w.shape[1]] = w
        out[D:, w.shape[1]:] = w
        return out

    def twice(v):
        return np.concatenate([v, v]).reshape(128, 1)

    cols = np.concatenate([
        twice(a["L0_tok_b_k"]), twice(a["L0_attn_bq"]), twice(a["L0_attn_bk"]), twice(a["L0_attn_bo"]),
        a["L0_ffn_b1"].T, a["L0_ffn_b2"].reshape(EPAIRS, 128).T, a["L0_tok_filt"].T, twice(a["L0_attn_bv"])], axis=1)
    qk0 = [a["L0_attn_bq"][0:1]] * 2 + [a["L0_attn_bk"][0:1]] * 2
    rows = np.concatenate([a["L0_ffn_bg"]] * CHUNKS + [a["L0_ffn_bias"]] * CHUNKS + qk0
                          + [np.arange(EXPERTS, dtype=np.float32)] * CHUNKS)
    arrays = {
        "xt": a["x"].reshape(GROUPS, PAIR, LEN, DIN).transpose(0, 3, 1, 2),
        "wtok": a["L0_tok_W_k"].reshape(TAPS, DIN, D).transpose(1, 0, 2),
        "cols": cols,
        "const": constants(),
        "wqk": np.concatenate([a["L0_attn_Wq"].T, a["L0_attn_Wk"].T], axis=1),
        "wv": a["L0_attn_Wv"],
        "wot": a["L0_attn_Wo"].T,
        "rows": np.tile(rows, (128, 1)),
        "bdg": diagonal(a["L0_ffn_Wg"]),
        "w1": a["L0_ffn_W1"].transpose(1, 0, 2),
        "w2": a["L0_ffn_W2"].transpose(1, 0, 2),
    }
    arrays = {k: np.ascontiguousarray(v) for k, v in arrays.items()}
    nc = bacc.Bacc("TRN2", target_bir_lowering=False, num_devices=1)
    aps = [nc.dram_tensor(k, v.shape, F32, kind="ExternalInput").ap() for k, v in arrays.items()]
    out = nc.dram_tensor("out", [GROUPS, 128, WIN], F32, kind="ExternalOutput").ap()
    weights_dram = nc.dram_tensor("weights", [EXPERTS, TOK], F32).ap()
    audio_tower(nc, *aps, out, weights_dram)
    r = run_bass_kernel_spmd(nc, [arrays], core_ids=[0])
    return r.results[0]["out"].reshape(SEQS, D, WIN).transpose(0, 2, 1)
```
